# Optimizing a Trainium2 kernel written in Bass

```python
import numpy as np
import jax
import jax.numpy as jnp

def _softmax(x, axis=-1):
    return jax.nn.softmax(x, axis=axis)
def _gelu(x):
    return jax.nn.gelu(x, approximate=True)
def _silu(x):
    return jax.nn.silu(x)
def _sigmoid(x):
    return jax.nn.sigmoid(x)
def _layernorm(x, axis=-1, eps=1e-5):
    m = jnp.mean(x, axis=axis, keepdims=True)
    v = jnp.var(x, axis=axis, keepdims=True)
    return (x - m) / jnp.sqrt(v + eps)
def _scatter_add(tgt, idx, src, axis=0):
    return tgt.at[idx].add(src)
def _segment_sum(src, seg, n):
    return jax.ops.segment_sum(src, seg, n)

kernel_name = 'mk_adj_resnorm_d4_adj_64_5292ba'

def setup_inputs(seed: int = 0):
    np.random.seed(seed)
    _w = jnp.asarray
    def _rec_inputs():
        import jax
        import jax.numpy as jnp
        _gk = jax.random.key(seed)
        x = -9.806e-05 + 1 * jax.random.normal(jax.random.fold_in(_gk, 1), (8192, 64), jnp.float32)
        _a = jax.random.bernoulli(jax.random.fold_in(_gk, 2), 0.000488281, (8192, 8192))
        _a = jnp.logical_or(_a, jnp.swapaxes(_a, -1, -2))
        _a = jnp.logical_or(_a, jnp.eye(8192, dtype=bool))
        adj = _a.astype(jnp.int32)
        return x, adj
    x, adj = _rec_inputs()
    def _L0_gnn_setup():
        import jax, jax.numpy as jnp
        import numpy as np
        ALPHA = 0.2
        NEG_BIG = -9000000000000000.0
        key = jax.random.key(seed)
        k1, k2, k3, k4, k5 = jax.random.split(key, 5)
        N, M, F_in, F_out = (8192, 8192, 64, 64)
        item_embs = jax.random.normal(k1, (N, F_in), dtype=jnp.float32)
        entity_embs = jax.random.normal(k2, (M, F_in), dtype=jnp.float32)
        adj = jax.random.randint(k3, (N, M), 0, 2, dtype=jnp.int32)
        W = jax.random.normal(k4, (F_in, F_out), dtype=jnp.float32)
        a = jax.random.normal(k5, (2 * F_out, 1), dtype=jnp.float32)
        return {'item_embs': item_embs, 'entity_embs': entity_embs, 'adj': adj, 'W': W, 'a': a}
    _L0_gnn_all = _L0_gnn_setup()
    _L0_gnn_in = {k: v for k, v in _L0_gnn_all.items() if k in ('entity_embs', 'W', 'a', )}
    del _L0_gnn_all

    def _L1_gnn_setup():
        import jax, jax.numpy as jnp
        import numpy as np
        ALPHA = 0.2
        NEG_INF = -9000000000000000.0
        key = jax.random.key(seed)
        k1, k2, k3, k4 = jax.random.split(key, 4)
        N, F_IN, F_OUT = (1024, 64, 64)
        h = jax.random.normal(k1, (N, F_IN), dtype=jnp.float32)
        adj = jax.random.randint(k2, (N, N), 0, 2, dtype=jnp.int32)
        lim_W = 1.414 * np.sqrt(6.0 / (F_IN + F_OUT))
        W = jax.random.uniform(k3, (F_IN, F_OUT), minval=-lim_W, maxval=lim_W, dtype=jnp.float32)
        lim_a = 1.414 * np.sqrt(6.0 / (2 * F_OUT + 1))
        a = jax.random.uniform(k4, (2 * F_OUT, 1), minval=-lim_a, maxval=lim_a, dtype=jnp.float32)
        return {'h': h, 'adj': adj, 'W': W, 'a': a}
    _L1_gnn_all = _L1_gnn_setup()
    _L1_gnn_in = {k: v for k, v in _L1_gnn_all.items() if k in ('W', 'a', )}
    del _L1_gnn_all

    def _L2_gnn_setup():
        import jax, jax.numpy as jnp
        import numpy as np
        N = 8192
        F_IN = 64
        F_OUT = 64
        NEG_SLOPE = 0.01
        MASK_FILL = -1000000000000.0
        key = jax.random.key(seed)
        k1, k2, k3, k4 = jax.random.split(key, 4)
        x = jax.random.normal(k1, (N, F_IN), dtype=jnp.float32)
        adj_matrix = jax.random.randint(k2, (N, N), 0, 2, dtype=jnp.int32)
        W = jax.random.normal(k3, (F_IN, F_OUT), dtype=jnp.float32) * (1.0 / np.sqrt(F_IN))
        a = jax.random.normal(k4, (2 * F_IN, 1), dtype=jnp.float32) * (1.0 / np.sqrt(2 * F_IN))
        return {'x': x, 'adj_matrix': adj_matrix, 'W': W, 'a': a}
    _L2_gnn_all = _L2_gnn_setup()
    _L2_gnn_in = {k: v for k, v in _L2_gnn_all.items() if k in ('W', 'a', )}
    del _L2_gnn_all

    def _L3_gnn_setup():
        import jax, jax.numpy as jnp
        import numpy as np
        N = 16384
        D = 64
        key = jax.random.key(seed)
        k1, k2, k3 = jax.random.split(key, 3)
        x = jax.random.normal(k1, (N, D), dtype=jnp.float32)
        adj_mat = jax.random.randint(k2, (N, N), 0, 2, dtype=jnp.int32)
        U = jax.random.normal(k3, (D, D), dtype=jnp.float32)
        return {'x': x, 'adj_mat': adj_mat, 'U': U}
    _L3_gnn_all = _L3_gnn_setup()
    _L3_gnn_in = {k: v for k, v in _L3_gnn_all.items() if k in ('U', )}
    del _L3_gnn_all

    return {
        "x": x,
        "adj": adj,
        "L0_gnn_entity_embs": _L0_gnn_in["entity_embs"],
        "L0_gnn_W": _L0_gnn_in["W"],
        "L0_gnn_a": _L0_gnn_in["a"],
        "L1_gnn_W": _L1_gnn_in["W"],
        "L1_gnn_a": _L1_gnn_in["a"],
        "L2_gnn_W": _L2_gnn_in["W"],
        "L2_gnn_a": _L2_gnn_in["a"],
        "L3_gnn_U": _L3_gnn_in["U"],
    }

def reference(x, adj, L0_gnn_entity_embs, L0_gnn_W, L0_gnn_a, L1_gnn_W, L1_gnn_a, L2_gnn_W, L2_gnn_a, L3_gnn_U):
    import jax
    import jax.numpy as jnp
    def _L0_gnn_ref(item_embs, entity_embs, adj, W, a):
        import jax, jax.numpy as jnp
        import numpy as np
        ALPHA = 0.2
        NEG_BIG = -9000000000000000.0
        F_out = W.shape[1]
        Wh = item_embs @ W
        We = entity_embs @ W
        a1 = a[:F_out, 0]
        a2 = a[F_out:, 0]
        scores = (Wh @ a1)[:, None] + (We @ a2)[None, :]
        e = jnp.where(scores > 0, scores, ALPHA * scores)
        e = jnp.where(adj > 0, e, NEG_BIG)
        attention = jax.nn.softmax(e, axis=1)
        entity_emb_weighted = attention @ entity_embs
        h_prime = entity_emb_weighted + item_embs
        return jax.nn.elu(h_prime)

    def _L1_gnn_ref(h, adj, W, a):
        import jax, jax.numpy as jnp
        import numpy as np
        ALPHA = 0.2
        NEG_INF = -9000000000000000.0
        F_OUT = W.shape[1]
        Wh = h @ W
        a1, a2 = (a[:F_OUT, 0], a[F_OUT:, 0])
        e = (Wh @ a1)[:, None] + (Wh @ a2)[None, :]
        e = jax.nn.leaky_relu(e, negative_slope=ALPHA)
        scores = jnp.where(adj > 0, e, jnp.float32(NEG_INF))
        attention = jax.nn.softmax(scores, axis=1)
        h_prime = attention @ Wh
        return jax.nn.elu(h_prime)

    def _L2_gnn_ref(x, adj_matrix, W, a):
        import jax, jax.numpy as jnp
        import numpy as np
        N = 8192
        F_IN = 64
        F_OUT = 64
        NEG_SLOPE = 0.01
        MASK_FILL = -1000000000000.0
        h = x @ W
        a1 = a[:F_OUT, 0]
        a2 = a[F_OUT:, 0]
        f1 = h @ a1
        f2 = h @ a2
        e = jax.nn.leaky_relu(f1[:, None] + f2[None, :], NEG_SLOPE)
        e = jnp.where(adj_matrix > 0, e, MASK_FILL)
        attention = jax.nn.softmax(e, axis=1)
        h_prime = attention @ h
        return jax.nn.elu(h_prime)

    def _L3_gnn_ref(x, adj_mat, U):
        import jax, jax.numpy as jnp
        import numpy as np
        N = 16384
        D = 64
        a = adj_mat.astype(x.dtype)
        deg = a.sum(axis=0)
        agg = jnp.einsum('ji,jd->id', a, x)
        out = jax.nn.relu(agg @ U.T / deg[:, None])
        return out

    x = _layernorm(x + _L0_gnn_ref(x, L0_gnn_entity_embs, adj, L0_gnn_W, L0_gnn_a), axis=-1)
    x = _layernorm(x + _L1_gnn_ref(x, adj, L1_gnn_W, L1_gnn_a), axis=-1)
    x = _layernorm(x + _L2_gnn_ref(x, adj, L2_gnn_W, L2_gnn_a), axis=-1)
    x = _layernorm(x + _L3_gnn_ref(x, adj, L3_gnn_U), axis=-1)
    return x


_drawn_inputs = setup_inputs


def setup_inputs(seed=0):
    import zlib

    import numpy as np

    out = dict(_drawn_inputs(seed))
    spreads = {}
    factors = {}
    for name, (base, spread) in spreads.items():
        noise = np.random.default_rng([zlib.crc32(name.encode()), seed]).standard_normal(out[name].shape)
        drawn = base * np.exp(spread * noise) if base else spread * noise
        out[name] = jnp.asarray(drawn.astype(out[name].dtype))
    for name, factor in factors.items():
        out[name] = (out[name] * factor).astype(out[name].dtype)
    return out
```

```python
from contextlib import ExitStack

import concourse.bass as bass
from concourse import mybir

ALU = mybir.AluOpType
ACT = mybir.ActivationFunctionType
AX_X = mybir.AxisListType.X
F32 = mybir.dt.float32
BF16 = mybir.dt.bfloat16
FP8 = mybir.dt.float8e4
I8 = mybir.dt.int8
I32 = mybir.dt.int32

P = 128
F = 64
FA = F + 1
SB = 8
W = SB * P
UN = 16
NQ = 4
GB = 4
NO_EDGE = -40
BIG = 2.0 ** 90
PARTS = 3
XP = PARTS * F + 1
TINY = 2.0 ** -100
EPS = 1e-5
SLOPES = (0.2, 0.2, 0.01)


def build(nc, x, adj, ent, W0, a0, W1, a1, W2, a2, UT, out):
    N = adj.shape[0]
    NB = N // P
    NS = N // W
    NP = NB // 2
    KT = NS * NB
    QW = N // NQ
    NG = NB // GB
    AHEAD = 5
    PQ = SB // 2
    fins3 = 3 * (NP - PQ + 1)
    CH_BASE = 3 * NS * NS // 2
    Ws, As = (W0, W1, W2), (a0, a1, a2)

    ctx = ExitStack()
    with ctx:
        def sb(name, shape, dt):
            return ctx.enter_context(nc.sbuf_tensor(name, shape, dt))

        def sem(name):
            return ctx.enter_context(nc.semaphore(name))

        mask_dram = nc.dram_tensor("mask_bytes", [N, N], I8, kind="Internal")
        mask_rows = mask_dram[:, :].rearrange("(r p) n -> r p n", p=P)
        mask_chunks = mask_dram[:, :].rearrange("(s b p) (c w) -> s c p b w", p=P, b=SB, w=W)
        adj_quarters = adj.rearrange("(r p) (c w) -> r c p w", p=P, w=QW)

        x_cur = sb("x_cur", [P, NB, F], F32)
        h_aug = sb("h_aug", [P, NB, FA], F32)
        t_row = sb("t_row", [P, N], F32)
        d_row = sb("d_row", [P, 2 * W], F32)
        s2_rows = sb("s2_rows", [P, 2 * W], BF16)
        ints = sb("ints", [P, NQ, QW], I32)
        rowmask = sb("rowmask", [P, 2, N], I8)
        chunk = sb("chunk", [P, 2, SB, W], I8)
        score = sb("score", [P, 2, W], F32)
        prob = sb("prob", [P, 2, W], F32)
        scrap = sb("scrap", [P, QW], BF16)
        ident = sb("ident", [P, P], F32)
        ident_b = sb("ident_b", [P, P], BF16)
        big_diag = sb("big_diag", [P, P], BF16)
        ones = sb("ones", [P, P], F32)
        ones_b = sb("ones_b", [P, P], BF16)
        zeros_b = sb("zeros_b", [P, 512], BF16)
        wgt = sb("wgt", [F, 3, F], F32)
        proj = sb("proj", [F, 3, F + 2], F32)
        ut = sb("ut", [F, F], F32)
        s_col = sb("s_col", [P, NB], F32)
        t_col = sb("t_col", [P, NB], F32)
        tn_col = sb("tn_col", [P, NB], F32)
        c_col = sb("c_col", [P, NB], F32)
        d_col = sb("d_col", [P, NB], F32)
        as_col = sb("as_col", [P, NB], F32)
        quarter_max = sb("quarter_max", [P, 2, NQ], F32)
        pair_max = sb("pair_max", [P, 2], F32)
        empty = sb("empty", [P, NB], F32)
        scale_col = sb("scale_col", [P, 1], F32)
        unscale = sb("unscale", [P, 1], F32)
        t_abs = sb("t_abs", [P, 1], F32)
        t_top = sb("t_top", [1, 2], F32)
        h_sum = sb("h_sum", [P, FA], F32)
        pr = sb("pr", [P, 12, 2], F32)
        s2_parts = sb("s2_parts", [P, 2, PARTS], BF16)
        d_diag = sb("d_diag", [P, 2, P], F32)
        h_tiles = sb("h_tiles", [P, 2, SB, FA], F32)
        acc_t = sb("acc_t", [FA, W], F32)
        acc_sb = sb("acc_sb", [P, SB, FA], F32)
        e_o = sb("e_o", [P, SB, F], F32)
        e_x = sb("e_x", [P, SB, F], F32)
        e_fill = sb("e_fill", [P, SB, FA], F32)
        e_small = sb("e_small", [P, 8, SB], F32)
        half = sb("half", [P, SB], F32)

        flat = score[:, :, :].rearrange("p a w -> p (a w)")
        stage = flat[:, 0:2 * GB * F].rearrange("p (i n) -> p i n", i=2)
        xt_sb = flat[0:F, 1024:2048].rearrange("p (i n) -> p i n", i=2)
        flat = prob[:, :, :].rearrange("p a w -> p (a w)")
        ht_sb = flat[0:F, 0:1024].rearrange("p (i n) -> p i n", i=2)
        t_diag = flat[:, 1024:2048].rearrange("p (i b n) -> p i b n", i=2, b=GB)

        x_parts = t_row[:, 0:NB * (XP + 1) // 2].bitcast(BF16).rearrange("p (b n) -> p b n", b=NB)
        adj_b = ints[:, :, :].rearrange("p i n -> p (i n)").bitcast(BF16).rearrange(
            "p (i b w) -> p i b w", i=2, b=SB)
        rest = h_aug[:, :, 0:F]
        acc3 = score[:, :, :].rearrange("p a w -> p (a w)")[:, 0:SB * XP].rearrange("p (b n) -> p b n", b=SB)
        agg_sb = prob[:, 0, 0:SB * F].rearrange("p (b n) -> p b n", b=SB)
        aggt_sb = prob[0:F, 1, :].rearrange("p (i n) -> p i n", i=2)

        z_ps = ctx.enter_context(nc.psum_tensor("z_ps", [P, 2, W], F32))
        acc_ps = ctx.enter_context(nc.psum_tensor("acc_ps", [P, 2, 512], F32))
        col_ps = ctx.enter_context(nc.psum_tensor("col_ps", [P, 512], F32))
        row_ps = ctx.enter_context(nc.psum_tensor("row_ps", [P, 512], F32))
        row_ps_b = row_ps[:, :].bitcast(BF16)
        edges8 = chunk[:, :, :, :].rearrange("p i b w -> p (i b w)").bitcast(FP8).rearrange(
            "p (i b w) -> p i b w", i=2, b=SB)
        z_flat = z_ps[:, :, :].rearrange("p a w -> p (a w)")
        turned = [bank[:, 0:SB // 2 * FA] for bank in (col_ps, row_ps)]

        PRIME = 2
        inputs_in = sem("inputs_in")
        consts_done = sem("consts_done")
        ident_step = sem("ident_step")
        consts_cast = sem("consts_cast")
        ints_in = [sem(f"ints_in{c}") for c in range(NQ)]
        bytes_done = sem("bytes_done")
        stored = [sem(f"stored{i}") for i in range(2)]
        rows_in = [sem(f"rows_in{i}") for i in range(2)]
        chunk_in = [sem(f"chunk_in{i}") for i in range(2)]
        pair_done = sem("pair_done")
        max_done = sem("max_done")
        stage_done = sem("stage_done")
        xt_ps_done = sem("xt_ps_done")
        xt_done = sem("xt_done")
        ht_ps_done = sem("ht_ps_done")
        ht_done = sem("ht_done")
        proj_ps_done = sem("proj_ps_done")
        proj_done = sem("proj_done")
        dve_step = sem("dve_step")
        abs_done = sem("abs_done")
        abs_t_done = sem("abs_t_done")
        top_done = sem("top_done")
        scale_ps_done = sem("scale_ps_done")
        diag_done = sem("diag_done")
        trow_ps_done = sem("trow_ps_done")
        trow_done = sem("trow_done")
        cols_done = sem("cols_done")
        hsum_ps_done = sem("hsum_ps_done")
        hsum_done = sem("hsum_done")
        pool_step = sem("pool_step")
        prep_done = sem("prep_done")
        prep_ps_done = sem("prep_ps_done")
        prep_rows_done = sem("prep_rows_done")
        mask_ps_done = sem("mask_ps_done")
        score_done = sem("score_done")
        exp_done = sem("exp_done")
        pv_done = sem("pv_done")
        acc_zero = sem("acc_zero")
        h_staged = sem("h_staged")
        acc_t_done = sem("acc_t_done")
        turned_done = sem("turned_done")
        acc_done = sem("acc_done")
        fixed = sem("fixed")
        recip_done = sem("recip_done")
        elu_in = sem("elu_in")
        elu_exp = sem("elu_exp")
        y_done = sem("y_done")
        sum_done = sem("sum_done")
        sq_done = sem("sq_done")
        var_done = sem("var_done")
        x_done = sem("x_done")
        parts_done = sem("parts_done")
        adj_done = sem("adj_done")
        adj_done_a = sem("adj_done_a")
        agg_step = sem("agg_step")
        agg_done = sem("agg_done")
        agg_sum = sem("agg_sum")
        aggt_ps_done = sem("aggt_ps_done")
        aggt_done = sem("aggt_done")
        lin_ps_done = sem("lin_ps_done")
        relu_done = sem("relu_done")
        out_in = sem("out_in")
        passed = {e.engine: sem(f"passed_{n}") for n, e in
                  (("sp", nc.sync), ("pool", nc.gpsimd), ("pe", nc.tensor), ("dve", nc.vector))}

        block = ctx.enter_context(nc.Block())

        def wait_alone(eng, which, value):
            eng.wait_ge(which, value)
            if not isinstance(value, int):
                eng.sem_inc(passed[eng.engine], 1)


        def layer_loop(eng, body, close, L):
            with eng.Fori(0, PQ) as q:
                body(q, True, True, False, False)
            close(0)
            with eng.Fori(1, NS - 2) as s:
                with eng.Fori(0, PQ) as r:
                    body(PQ * s + r, True, True, True, False)
                close(s)
            with eng.Fori(NP - 2 * PQ, NP - AHEAD) as q:
                body(q, True, True, True, False)
            body(NP - AHEAD, False, True, True, False)
            close(NS - 2)
            with eng.Fori(NP - PQ, NP - 1) as q:
                body(q, False, False, True, False)
            body(NP - 1, False, False, True, True)
            close(NS - 1)

        PROJ = {0: (0, 1), 1: (2,), 2: (3,)}

        @block.sync
        def _(sp):
            sp.dma_start(h_aug[:, :, 0:F], ent.rearrange("(b p) f -> p b f", p=P)).then_inc(inputs_in, 16)
            sp.dma_start(x_cur[:, :, :], x.rearrange("(b p) f -> p b f", p=P)).then_inc(inputs_in, 16)
            for l in range(3):
                sp.dma_start(wgt[:, l, :], Ws[l]).then_inc(inputs_in, 16)
                sp.dma_start(proj[:, l, F:F + 1], As[l][0:F, :]).then_inc(inputs_in, 16)
                sp.dma_start(proj[:, l, F + 1:F + 2], As[l][F:2 * F, :]).then_inc(inputs_in, 16)
            sp.dma_start(ut[:, :], UT).then_inc(inputs_in, 16)

            def load_ints(r, c):
                wait_alone(sp, bytes_done, NQ * r + c + 1)
                sp.dma_start(ints[:, c, :], adj_quarters[bass.ds(r, 1), c, :, :].rearrange("a p w -> (a p) w"))\
                  .then_inc(ints_in[c], 16)

            def store_rows(r, i):
                wait_alone(sp, bytes_done, NQ + NQ * r + NQ)
                sp.dma_start(mask_rows[bass.ds(r, 1), :, :].rearrange("a p n -> (a p) n"), rowmask[:, i, :])\
                  .then_inc(stored[i], 16)

            def load_rows(L, r, i):
                wait_alone(sp, max_done, NB * NQ * L + NQ * r + NQ)
                sp.dma_start(rowmask[:, i, :], mask_rows[bass.ds(r, 1), :, :].rearrange("a p n -> (a p) n"))\
                  .then_inc(rows_in[i], 16)

            def load_chunk(L, g, i):
                sp.dma_start(chunk[:, i, :, :], mask_chunks[bass.ds(g // NS, 1), bass.ds(g % NS, 1), :, :, :]
                             .rearrange("s c p b w -> (s c p) b w")).then_inc(chunk_in[i], 16)

            for c in range(NQ):
                load_ints(0, c)
            with sp.Fori(0, AHEAD) as pair:
                for i in range(2):
                    for c in range(NQ):
                        load_ints(2 * pair + i + 1, c)
                    store_rows(2 * pair + i, i)

            def all_stored(upto):
                for i in range(2):
                    wait_alone(sp, stored[i], 16 * upto)

            for L in range(3):
                if L > 0:
                    load_rows(L, 0, 0)
                    with sp.Fori(0, AHEAD) as pair:
                        load_rows(L, 2 * pair + 1, 1)
                        load_rows(L, 2 * pair + 2, 0)
                    wait_alone(sp, mask_ps_done, KT * L)
                else:
                    all_stored(PQ)
                load_chunk(L, 0, 0)

                def body(q, row_max_on, prepare, finish, last):
                    for i in range(2):
                        g = 2 * q + i
                        if not (last and i == 1):
                            if L == 0:
                                all_stored(q + AHEAD if row_max_on else NP)
                            wait_alone(sp, mask_ps_done, KT * L + SB * g)
                            load_chunk(L, g + 1, (i + 1) % 2)
                        if row_max_on:
                            r = 2 * (q + AHEAD) + i
                            final = isinstance(q, int) and q == NP - AHEAD - 1 and i == 1
                            if L == 0:
                                if not final:
                                    for c in range(NQ):
                                        load_ints(r + 1, c)
                                store_rows(r, i)
                            elif not final:
                                load_rows(L, r + 1, (i + 1) % 2)

                with sp.Fori(0, NP - AHEAD - 1) as q:
                    body(q, True, True, True, False)
                body(NP - AHEAD - 1, True, True, True, False)
                with sp.Fori(NP - AHEAD, NP - 1) as q:
                    body(q, False, False, True, False)
                body(NP - 1, False, False, True, True)

            wait_alone(sp, mask_ps_done, KT * 3)
            with sp.Fori(0, NS) as jc:
                with sp.Fori(0, NS // 2) as s2:
                    for i in range(2):
                        g = NS * jc + 2 * s2 + i
                        wait_alone(sp, adj_done, g + 1)
                        wait_alone(sp, adj_done_a, g + 1)
                        sp.dma_start(chunk[:, i, :, :], mask_chunks[bass.ds(2 * s2 + i, 1), bass.ds(jc, 1), :, :, :]
                                     .rearrange("s c p b w -> (s c p) b w")).then_inc(chunk_in[i], 16)
            wait_alone(sp, x_done, fins3 + NS)
            sp.dma_start(out.rearrange("(b p) f -> p b f", p=P), x_cur[:, :, :]).then_inc(out_in, 16)
            sp.wait_ge(out_in, 16)

        @block.gpsimd
        def _(pool):
            pool.memset(s2_rows[:, :], 0.0).then_inc(consts_done, 1)
            pool.memset(ident[:, :], 0.0).then_inc(ident_step, 1)
            pool.memset(ones[:, :], 1.0).then_inc(consts_done, 1)
            pool.memset(ones_b[:, :], 1.0).then_inc(consts_done, 1)
            pool.memset(zeros_b[:, :], 0.0).then_inc(consts_done, 1)
            pool.memset(half[:, :], -0.5).then_inc(consts_done, 1)
            pool.memset(h_aug[:, :, F:FA], 1.0).then_inc(consts_done, 1)
            pool.wait_ge(ident_step, 1)
            pool.affine_select(out=ident[:, :], in_=ident[:, :], compare_op=ALU.not_equal, fill=1.0, base=0,
                               pattern=[[-1, P]], channel_multiplier=1).then_inc(consts_done, 1)
            pool.wait_ge(inputs_in, 16 * 12)
            def stage_group(n, g, i, src):
                wait_alone(pool, xt_ps_done, NG * n + g + 1)
                pool.tensor_copy(stage[:, i, :].rearrange("p (b f) -> p b f", b=GB),
                                 src[:, bass.ds(GB * g, GB), 0:F]).then_inc(stage_done, 1)

            def prepare_pair(L, pi, steps):
                a = SLOPES[L]
                n = [0]

                def then(ins):
                    n[0] += 1
                    ins.then_inc(pool_step, 1)
                    wait_alone(pool, pool_step, steps + n[0])
                cols = bass.ds(2 * pi, 2)
                wait_alone(pool, pair_done, NP * L + pi + 1)
                none = pr[:, 11, :]
                (edge, m1, m2, y, up, low, m, s2, r1, r2) = (pr[:, k, :] for k in range(10))
                then(pool.tensor_scalar(none, pair_max[:, :], NO_EDGE / 2, None, ALU.is_lt))
                then(pool.tensor_copy(empty[:, cols], none))
                then(pool.tensor_scalar(edge, none, -1.0, 1.0, ALU.mult, ALU.add))
                then(pool.tensor_tensor(m1, pair_max[:, :], edge, ALU.mult))
                then(pool.tensor_scalar(m2, m1, scale_col[:, 0:1], None, ALU.mult))
                then(pool.tensor_tensor(y, m2, s_col[:, cols], ALU.add))
                then(pool.tensor_scalar(up, y, 0.0, 1.0 - a, ALU.max, ALU.mult))
                then(pool.tensor_scalar(low, y, a, None, ALU.mult))
                then(pool.tensor_tensor(m, up, low, ALU.add))
                then(pool.tensor_tensor(s2, as_col[:, cols], m, ALU.subtract))
                wait_alone(pool, prep_ps_done, NP * L + pi)
                then(pool.tensor_copy(s2_parts[:, :, 0], s2))
                then(pool.tensor_tensor(r1, s2, s2_parts[:, :, 0], ALU.subtract))
                then(pool.tensor_copy(s2_parts[:, :, 1], r1))
                then(pool.tensor_tensor(r2, r1, s2_parts[:, :, 1], ALU.subtract))
                then(pool.tensor_copy(s2_parts[:, :, 2], r2))
                then(pool.tensor_tensor(d_diag[:, :, :], ident[:, :].unsqueeze(1).to_broadcast([P, 2, P]),
                                        d_col[:, cols].unsqueeze(2).to_broadcast([P, 2, P]), ALU.mult))
                pool.tensor_copy(pr[:, 10, :], r2).then_inc(prep_done, 1)
                return n[0]

            def finish_rows(L, first, lo, nb, count, steps):
                n = [0]

                def then(ins):
                    n[0] += 1
                    ins.then_inc(pool_step, 1)
                    wait_alone(pool, pool_step, steps + n[0])
                rows, part = bass.ds(first, nb), bass.ds(lo, nb)
                acc, o, ex = acc_sb[:, part, :], e_o[:, 0:nb, :], e_x[:, 0:nb, :]
                fill = e_fill[:, 0:nb, :]
                rz, sm, mu, vs, v1, rs = (e_small[:, k, 0:nb] for k in range(6))

                def wide(col, w=F):
                    return col.unsqueeze(2).to_broadcast([P, nb, w])
                then(pool.tensor_tensor(fill, h_sum[:, :].unsqueeze(1).to_broadcast([P, nb, FA]),
                                        wide(empty[:, rows], FA), ALU.mult))
                then(pool.tensor_tensor(acc, acc, fill, ALU.add))
                pool.tensor_copy(e_small[:, 6, 0:nb], acc[:, :, F]).then_inc(fixed, 1)
                wait_alone(pool, recip_done, count + 1)
                then(pool.tensor_tensor(o, acc[:, :, 0:F], wide(rz), ALU.mult))
                if L == 0:
                    then(pool.tensor_tensor(o, o, x_cur[:, rows, :], ALU.add))
                pool.tensor_scalar(ex, o, 0.0, None, ALU.min).then_inc(elu_in, 1)
                then(pool.tensor_scalar(o, o, 0.0, -1.0, ALU.max, ALU.add))
                then(pool.tensor_tensor(o, o, x_cur[:, rows, :], ALU.add))
                wait_alone(pool, elu_exp, count + 1)
                pool.tensor_tensor(o, o, ex, ALU.add).then_inc(y_done, 1)
                normalise(then, rows, nb, count)
                return n[0]

            def normalise(then, rows, nb, count, extra=None):
                o, ex = e_o[:, 0:nb, :], e_x[:, 0:nb, :]
                rz, sm, mu, vs, v1, rs = (e_small[:, k, 0:nb] for k in range(6))

                def wide(col):
                    return col.unsqueeze(2).to_broadcast([P, nb, F])
                wait_alone(pool, sum_done, count + 1)
                then(pool.tensor_scalar(mu, sm, -1.0 / F, None, ALU.mult))
                if extra is not None:
                    then(pool.tensor_tensor(mu, mu, extra, ALU.add))
                then(pool.tensor_tensor(o, o, wide(mu), ALU.add))
                pool.tensor_tensor(ex, o, o, ALU.mult).then_inc(sq_done, 1)
                wait_alone(pool, var_done, count + 1)
                then(pool.tensor_scalar(v1, vs, 1.0 / F, EPS, ALU.mult, ALU.add))
                then(pool.tensor_tensor(rs, v1, half[:, 0:nb], ALU.pow))
                pool.tensor_tensor(x_cur[:, rows, :], o, wide(rs), ALU.mult).then_inc(x_done, 1)

            PREP = 16
            steps = 0
            for L in range(3):
                FIN_L = 2 + (2 if L == 0 else 1) + 2 + 2 + 2
                base = steps
                sources = (h_aug, x_cur) if L == 0 else (x_cur,)
                if L > 0:
                    wait_alone(pool, x_done, (NP - PQ + 1) * L)
                    wait_alone(pool, pv_done, PRIME + KT * L)
                for n, src in zip(PROJ[L], sources):
                    with pool.Fori(0, NG // 2) as g2:
                        for i in range(2):
                            stage_group(n, 2 * g2 + i, i, src)
                wait_alone(pool, cols_done, L + 1)
                with pool.Fori(0, PQ) as pi:
                    assert prepare_pair(L, pi, base + PREP * pi) == PREP
                base += PREP * PQ
                fins = (NP - PQ + 1) * L

                def body(q, row_max_on, prepare, finish, last, L=L, base=base, fins=fins):
                    if prepare:
                        if finish:
                            before = base + PREP * q + FIN_L * (q - PQ)
                        else:
                            before = base + PREP * q
                        prepare_pair(L, q + PQ, before)
                        before = before + PREP
                    else:
                        before = base + PREP * (NP - PQ) + FIN_L * (q - PQ)
                    if finish:
                        lo = 2 * (q % PQ)
                        wait_alone(pool, acc_done, 2 * (NS * L) + 2 * (q // PQ))
                        assert finish_rows(L, 2 * (q - PQ), lo, 2, fins + q - PQ, before) == FIN_L

                wait_alone(pool, hsum_done, L + 1)
                layer_loop(pool, body, lambda s: None, L)
                base += PREP * (NP - PQ) + FIN_L * (NP - PQ)
                wait_alone(pool, acc_done, 2 * NS * (L + 1))
                assert finish_rows(L, NB - SB, 0, SB, fins + NP - PQ, base) == FIN_L
                base += FIN_L
                steps = base

            fins = 3 * (NP - PQ + 1)
            AGG = 1
            FIN3 = 5
            with pool.Fori(0, NS) as jc:
                before = steps + (AGG + FIN3) * jc
                n = [0]

                def then(ins):
                    n[0] += 1
                    ins.then_inc(pool_step, 1)
                    wait_alone(pool, pool_step, before + n[0])
                wait_alone(pool, agg_done, 4 * jc + 4)
                then(pool.tensor_tensor(acc3[:, :, F:2 * F], acc3[:, :, F:2 * F], acc3[:, :, 2 * F:3 * F], ALU.add))
                pool.tensor_tensor(agg_sb, acc3[:, :, 0:F], acc3[:, :, F:2 * F], ALU.add).then_inc(agg_sum, 1)
                wait_alone(pool, relu_done, jc + 1)
                normalise(then, bass.ds(SB * jc, SB), SB, fins + jc, extra=e_small[:, 6, :])
                assert n[0] == AGG + FIN3

        @block.scalar
        def _(act):
            act.wait_ge(inputs_in, 16 * 12)
            act.sem_inc(bytes_done, NQ)
            act.sem_inc(exp_done, PRIME)
            act.sem_inc(ht_done, PRIME)
            act.sem_inc(trow_done, PRIME)

            def to_bytes(r, c, i):
                act.wait_ge(ints_in[c], 16 * (r + 1))
                act.wait_ge(max_done, NQ * r + c + 1)
                act.wait_ge(stored[i], 16 * (r // 2))
                act.activation(rowmask[:, i, c * QW:(c + 1) * QW], ints[:, c, :], ACT.Copy,
                               bias=float(NO_EDGE), scale=-float(NO_EDGE)).then_inc(bytes_done, 1)

            def copy_prepared(L, pi):
                act.wait_ge(prep_ps_done, NP * L + pi + 1)
                act.activation(d_row[:, bass.ds(2 * P * (pi % (2 * PQ)), 2 * P)], col_ps[:, 0:2 * P], ACT.Copy)\
                   .then_inc(prep_rows_done, 1)
                act.activation(s2_rows[0:PARTS, bass.ds(2 * P * (pi % (2 * PQ)), 2 * P)], row_ps_b[0:PARTS, 0:2 * P], ACT.Copy)\
                   .then_inc(prep_rows_done, 1)

            for L in range(3):
                for n in PROJ[L]:
                    with act.Fori(0, NG // 2) as g2:
                        for i in range(2):
                            g = 2 * g2 + i
                            act.wait_ge(ht_ps_done, PRIME + NG * n + g + 1)
                            act.wait_ge(proj_ps_done, NG * n + g + 1)
                            act.activation(ht_sb[:, i, :], z_ps[0:F, 1, 512 * i:512 * i + 512], ACT.Copy)\
                               .then_inc(ht_done, 1)
                with act.Fori(0, NG // 2) as g2:
                    for i in range(2):
                        g = 2 * g2 + i
                        act.wait_ge(trow_ps_done, PRIME + NG * L + g + 1)
                        act.activation(t_row[:, bass.ds(512 * g, 512)], z_ps[:, 0, 512 * i:512 * i + 512],
                                       ACT.Copy).then_inc(trow_done, 1)
                act.wait_ge(hsum_ps_done, L + 1)
                act.activation(h_sum[:, :], acc_ps[:, 0, 0:FA], ACT.Copy).then_inc(hsum_done, 1)
                if L == 0:
                    for i in range(2):
                        for c in range(NQ):
                            to_bytes(i, c, i)
                    with act.Fori(1, AHEAD) as pair:
                        for i in range(2):
                            for c in range(NQ):
                                to_bytes(2 * pair + i, c, i)
                        copy_prepared(L, pair - 1)
                else:
                    with act.Fori(0, PQ) as pi:
                        copy_prepared(L, pi)
                fins = (NP - PQ + 1) * L

                def stage_h(g, i):
                    act.activation(h_tiles[:, i, :, :], h_aug[:, bass.ds(SB * (g % NS), SB), :], ACT.Copy)\
                       .then_inc(h_staged, 1)

                act.wait_ge(pv_done, PRIME + KT * L)
                stage_h(0, 0)

                def elu(nb, count):
                    act.wait_ge(elu_in, count + 1)
                    act.activation(e_x[:, 0:nb, :], e_x[:, 0:nb, :], ACT.Exp).then_inc(elu_exp, 1)

                def body(q, row_max_on, prepare, finish, last, L=L, fins=fins):
                    for u in range(UN):
                        k = UN * q + u
                        act.wait_ge(score_done, PRIME + KT * L + k + 1)
                        act.wait_ge(pv_done, KT * L + k + 1)
                        act.activation(prob[:, u % 2, :], score[:, u % 2, :], ACT.Exp,
                                       bias=t_col[:, bass.ds(k % NB, 1)]).then_inc(exp_done, 1)
                        if u == 1:
                            stage_h(2 * q + 1, 1)
                        if u == SB + 1 and not last:
                            stage_h(2 * q + 2, 0)
                        if L == 0 and row_max_on and u % 2:
                            i, c = u // SB, (u % SB) // 2
                            to_bytes(2 * (q + AHEAD) + i, c, i)
                        if prepare and u == 10:
                            copy_prepared(L, q + PQ)
                        if finish and u == 6:
                            elu(2, fins + q - PQ)

                def close(s, L=L, fins=fins):
                    act.wait_ge(pv_done, PRIME + KT * L + NB * (s + 1))
                    act.wait_ge(x_done, fins + PQ * s)
                    for i in range(2):
                        act.activation(acc_t[:, 512 * i:512 * i + 512], acc_ps[0:FA, i, :], ACT.Copy)\
                           .then_inc(acc_t_done, 1)
                    for i in range(2):
                        act.wait_ge(turned_done, 2 * (NS * L + s) + i + 1)
                        act.activation(acc_sb[:, SB // 2 * i:SB // 2 * (i + 1), :],
                                       turned[i].rearrange("p (b f) -> p b f", b=SB // 2),
                                       ACT.Copy).then_inc(acc_done, 1)

                layer_loop(act, body, close, L)
                elu(SB, fins + NP - PQ)

            act.sem_inc(adj_done_a, PRIME)
            with act.Fori(0, NS) as jc:
                with act.Fori(0, NS // 2) as s2:
                    for i in range(2):
                        g = NS * jc + 2 * s2 + i
                        act.wait_ge(chunk_in[i], 16 * (CH_BASE + (NS // 2) * jc + s2 + 1))
                        act.wait_ge(agg_step, g + 1)
                        act.activation(adj_b[:, i, 0:SB // 2, :], chunk[:, i, 0:SB // 2, :], ACT.Relu, bias=1.0).then_inc(adj_done_a, 1)
                act.wait_ge(agg_step, PRIME + NS * jc + NS)
                act.wait_ge(x_done, fins3 + jc)
                for i in range(4):
                    act.activation(acc3[:, 2 * i:2 * i + 2, :],
                                   z_flat[:, 512 * i:512 * i + 2 * XP].rearrange("p (b n) -> p b n", b=2),
                                   ACT.Copy).then_inc(agg_done, 1)
                for i in range(2):
                    act.wait_ge(aggt_ps_done, 2 * jc + i + 1)
                    act.activation(aggt_sb[:, i, :], acc_ps[0:F, i, :], ACT.Copy).then_inc(aggt_done, 1)

        @block.vector
        def _(dve):
            dve.sem_inc(max_done, 2 * NQ)
            dve.sem_inc(xt_done, PRIME)
            dve.sem_inc(proj_done, PRIME)
            dve.sem_inc(score_done, PRIME)
            dve.wait_ge(consts_done, 7)
            dve.wait_ge(inputs_in, 16 * 12)
            dve.tensor_copy(ident_b[:, :], ident[:, :]).then_inc(consts_cast, 1)
            dve.tensor_scalar(big_diag[:, :], ident[:, :], BIG, None, ALU.mult).then_inc(consts_cast, 1)
            for l in range(3):
                dve.tensor_copy(proj[:, l, 0:F], ident[0:F, 0:F]).then_inc(consts_cast, 1)
            steps = [0]

            def then(ins):
                steps[0] += 1
                ins.then_inc(dve_step, 1)
                dve.wait_ge(dve_step, steps[0])

            def row_max_quarter(L, r, c, i):
                if L == 0:
                    wait_alone(dve, bytes_done, NQ + NQ * r + c + 1)
                elif c == 0:
                    wait_alone(dve, rows_in[i], 16 * ((NB // 2) * (L - 1) + r // 2 + 1))
                wait_alone(dve, max_done, 2 * NQ + NB * NQ * L + NQ * r + c)
                start = quarter_max[:, i, c - 1:c] if c else -3.0e38
                dve.tensor_tensor_reduce(scrap[:, :], rowmask[:, i, c * QW:(c + 1) * QW],
                                         t_row[:, c * QW:(c + 1) * QW], 1.0, start, ALU.add, ALU.max,
                                         quarter_max[:, i, c:c + 1]).then_inc(max_done, 1)

            def pair_max_out(L, pair):
                dve.wait_ge(max_done, 2 * NQ + NB * NQ * L + 2 * NQ * (pair + 1))
                dve.wait_ge(prep_done, NP * L + pair)
                dve.tensor_copy(pair_max[:, :], quarter_max[:, :, NQ - 1]).then_inc(pair_done, 1)

            for L in range(3):
                a = SLOPES[L]
                if L > 0:
                    dve.wait_ge(pv_done, PRIME + KT * L)
                    dve.wait_ge(prep_done, NP * L)
                for n in PROJ[L]:
                    with dve.Fori(0, NG // 2) as g2:
                        for i in range(2):
                            g = 2 * g2 + i
                            dve.wait_ge(xt_ps_done, PRIME + NG * n + g + 1)
                            dve.wait_ge(ht_ps_done, NG * n + g + 1)
                            dve.tensor_copy(xt_sb[:, i, :], z_ps[0:F, 0, 512 * i:512 * i + 512]).then_inc(xt_done, 1)
                        for i in range(2):
                            g = 2 * g2 + i
                            rows = bass.ds(GB * g, GB)
                            dve.wait_ge(proj_ps_done, PRIME + NG * n + g + 1)
                            got = acc_ps[:, i, 0:GB * (F + 2)].rearrange("p (b f) -> p b f", b=GB)
                            if L > 0:
                                dve.tensor_copy(h_aug[:, rows, 0:F], got[:, :, 0:F])
                            if n != 0:
                                last = dve.tensor_copy(s_col[:, rows], got[:, :, F])
                            if n != 1:
                                last = dve.tensor_copy(t_col[:, rows], got[:, :, F + 1])
                            last.then_inc(proj_done, 1)
                dve.wait_ge(proj_done, PRIME + NG * (PROJ[L][-1] + 1))
                dve.tensor_scalar(d_col[:, :], s_col[:, :], 1.0 - a, None, ALU.mult)
                dve.tensor_scalar(as_col[:, :], s_col[:, :], a, None, ALU.mult)
                dve.tensor_scalar(c_col[:, :], t_col[:, :], a - 1.0, None, ALU.mult)
                dve.tensor_reduce(t_abs[:, :], t_col[:, :], AX_X, ALU.max, apply_absolute_value=True)\
                   .then_inc(abs_done, 1)
                dve.wait_ge(abs_t_done, L + 1)
                then(dve.tensor_reduce(t_top[:, 0:1], col_ps[0:1, 0:P], AX_X, ALU.max))
                then(dve.tensor_scalar(t_top[:, 0:1], t_top[:, 0:1], TINY, None, ALU.max))
                dve.tensor_scalar(t_top[:, 1:2].bitcast(I32), t_top[:, 0:1].bitcast(I32), 0x7F800000, None,
                                  ALU.bitwise_and).then_inc(top_done, 1)
                dve.wait_ge(scale_ps_done, L + 1)
                then(dve.tensor_copy(scale_col[:, :], col_ps[:, 256:257]))
                then(dve.reciprocal(unscale[:, :], scale_col[:, :]))
                then(dve.tensor_scalar(tn_col[:, :], t_col[:, :], unscale[:, 0:1], None, ALU.mult))
                dve.memset(e_small[:, 7, :], 0.0).then_inc(cols_done, 1)
                with dve.Fori(0, NG // 2) as g2:
                    for i in range(2):
                        g = 2 * g2 + i
                        dve.wait_ge(trow_ps_done, NG * L + g + 1)
                        dve.tensor_tensor(t_diag[:, i, :, :], ident[:, :].unsqueeze(1).to_broadcast([P, GB, P]),
                                          tn_col[:, bass.ds(GB * g, GB)].unsqueeze(2).to_broadcast([P, GB, P]),
                                          ALU.mult).then_inc(diag_done, 1)
                dve.wait_ge(trow_done, PRIME + NG * (L + 1))
                with dve.Fori(0, AHEAD) as pair:
                    for i in range(2):
                        for c in range(NQ):
                            row_max_quarter(L, 2 * pair + i, c, i)
                    pair_max_out(L, pair)
                fins = (NP - PQ + 1) * L

                def recip(nb, count):
                    dve.wait_ge(fixed, count + 1)
                    dve.reciprocal(e_small[:, 0, 0:nb], e_small[:, 6, 0:nb]).then_inc(recip_done, 1)

                def sums(nb, count):
                    dve.wait_ge(y_done, count + 1)
                    dve.tensor_reduce(e_small[:, 1, 0:nb], e_o[:, 0:nb, :], AX_X, ALU.add).then_inc(sum_done, 1)

                def squares(nb, count):
                    dve.wait_ge(sq_done, count + 1)
                    dve.tensor_reduce(e_small[:, 3, 0:nb], e_x[:, 0:nb, :], AX_X, ALU.add).then_inc(var_done, 1)

                def body(q, row_max_on, prepare, finish, last, L=L, fins=fins):
                    for u in range(UN):
                        k = UN * q + u
                        dve.wait_ge(mask_ps_done, KT * L + k + 1)
                        dve.wait_ge(exp_done, KT * L + k + 1)
                        dve.scalar_tensor_tensor(out=score[:, u % 2, :], in0=d_row[:, bass.ds(W * (q // PQ % 2), W)],
                                                 scalar=c_col[:, bass.ds(k % NB, 1)], in1=z_ps[:, u % 2, :],
                                                 op0=ALU.max, op1=ALU.add).then_inc(score_done, 1)
                        if row_max_on and u % 2:
                            i, c = u // SB, (u % SB) // 2
                            row_max_quarter(L, 2 * (q + AHEAD) + i, c, i)
                        if finish:
                            count = fins + q - PQ
                            if u == 4:
                                recip(2, count)
                            if u == 9:
                                sums(2, count)
                            if u == 13:
                                squares(2, count)
                    if row_max_on:
                        pair_max_out(L, q + AHEAD)

                layer_loop(dve, body, lambda s: None, L)
                recip(SB, fins + NP - PQ)
                sums(SB, fins + NP - PQ)
                squares(SB, fins + NP - PQ)

            dve.sem_inc(adj_done, PRIME)
            dve.wait_ge(x_done, fins3)
            dve.wait_ge(max_done, 2 * NQ + 3 * NB * NQ)
            parts = [x_parts[:, :, F * k:F * k + F] for k in range(PARTS)]
            then(dve.memset(x_parts[:, :, PARTS * F:XP], 1.0))
            then(dve.tensor_copy(parts[0], x_cur[:, :, :]))
            then(dve.tensor_tensor(rest, x_cur[:, :, :], parts[0], ALU.subtract))
            then(dve.tensor_copy(parts[1], rest))
            then(dve.tensor_tensor(rest, rest, parts[1], ALU.subtract))
            dve.tensor_copy(parts[2], rest).then_inc(parts_done, 1)
            base = steps[0]
            with dve.Fori(0, NS) as jc:
                with dve.Fori(0, NS // 2) as s2:
                    for i in range(2):
                        g = NS * jc + 2 * s2 + i
                        dve.wait_ge(chunk_in[i], 16 * (CH_BASE + (NS // 2) * jc + s2 + 1))
                        dve.wait_ge(agg_step, g + 1)
                        dve.tensor_scalar(adj_b[:, i, SB // 2:SB, :], chunk[:, i, SB // 2:SB, :], 0.0, None,
                                          ALU.is_ge).then_inc(adj_done, 1)
                count = fins3 + jc
                dve.wait_ge(agg_done, 4 * jc + 4)
                dve.reciprocal(e_small[:, 0, :], acc3[:, :, PARTS * F]).then_inc(dve_step, 1)
                dve.wait_ge(dve_step, base + 2 * jc + 1)
                dve.tensor_scalar(e_small[:, 6, :], e_small[:, 0, :], 0.0, None, ALU.mult)
                dve.wait_ge(lin_ps_done, jc + 1)
                dve.tensor_tensor(e_o[:, :, :], col_ps[:, :].rearrange("p (b f) -> p b f", b=SB),
                                  e_small[:, 0, :].unsqueeze(2).to_broadcast([P, SB, F]), ALU.mult)\
                   .then_inc(dve_step, 1)
                dve.wait_ge(dve_step, base + 2 * jc + 2)
                dve.scalar_tensor_tensor(out=e_o[:, :, :], in0=e_o[:, :, :], scalar=0.0,
                                         in1=x_cur[:, bass.ds(SB * jc, SB), :], op0=ALU.max, op1=ALU.add)\
                   .then_inc(relu_done, 1)
                dve.wait_ge(relu_done, jc + 1)
                dve.tensor_reduce(e_small[:, 1, :], e_o[:, :, :], AX_X, ALU.add).then_inc(sum_done, 1)
                dve.wait_ge(sq_done, count + 1)
                dve.tensor_reduce(e_small[:, 3, :], e_x[:, :, :], AX_X, ALU.add).then_inc(var_done, 1)

        @block.tensor
        def _(pe):
            pe.sem_inc(xt_ps_done, PRIME)
            pe.sem_inc(ht_ps_done, PRIME)
            pe.sem_inc(proj_ps_done, PRIME)
            pe.sem_inc(trow_ps_done, PRIME)
            pe.sem_inc(pv_done, PRIME)
            pe.sem_inc(agg_step, PRIME)
            pe.wait_ge(consts_cast, 5)

            def prepare_rows(L, pi, closed):
                pe.wait_ge(prep_done, NP * L + pi + 1)
                pe.wait_ge(prep_rows_done, 2 * (NP * L + pi))
                pe.wait_ge(acc_done, 2 * (NS * L + closed))
                pe.matmul(col_ps[:, 0:2 * P], ones[:, :], d_diag[:, :, :].rearrange("p b n -> p (b n)"),
                          start=True, stop=True)
                for b in range(2):
                    last = pe.transpose(row_ps_b[0:PARTS, P * b:P * b + P], s2_parts[:, b, :], ident_b[:, :])
                last.then_inc(prep_ps_done, 1)

            def mask_tile(L, q, u, first_of_chunk):
                k = UN * q + u
                if first_of_chunk:
                    wait_alone(pe, chunk_in[u // SB], 16 * ((NS * NS // 2) * L + q + 1))
                wait_alone(pe, score_done, KT * L + k + 1)
                for w in range(0, W, 512):
                    bank = z_ps[:, u % 2, w:w + 512]
                    pe.matmul(bank, ones_b[:, :], s2_rows[:, bass.ds(W * (q // PQ % 2) + w, 512)], start=True, stop=False)
                    for b in range(w // P, w // P + 512 // P):
                        last = pe.matmul(z_ps[:, u % 2, P * b:P * b + P],
                                         edges8[:, u // SB, b, P * (u % SB):P * (u % SB) + P], big_diag[:, :],
                                         start=False, stop=(P * b + P == w + 512))
                last.then_inc(mask_ps_done, 1)

            def add_tile(L, q, u):
                k = UN * q + u
                if u % SB == 0:
                    wait_alone(pe, h_staged, NS * NS * L + 2 * q + u // SB + 1)
                pe.wait_ge(exp_done, PRIME + KT * L + k + 1)
                for i in range(2):
                    last = pe.matmul(acc_ps[0:FA, i, :], h_tiles[:, u // SB, u % SB, :],
                                     prob[:, u % 2, 512 * i:512 * i + 512], start=False, stop=False,
                                     skip_group_check=True)
                last.then_inc(pv_done, 1)

            def clear(banks, width):
                for bank in banks:
                    pe.matmul(bank, zeros_b[:, 0:bank.shape[0]], zeros_b[:, 0:width], start=True, stop=False,
                              skip_group_check=True)

            for L in range(3):
                for n in PROJ[L]:
                    l = L
                    with pe.Fori(0, NG // 2) as g2:
                        for i in range(2):
                            g = 2 * g2 + i
                            wait_alone(pe, stage_done, NG * n + g + 1)
                            wait_alone(pe, xt_done, NG * n + g + 1)
                            for b in range(GB):
                                last = pe.transpose(z_ps[0:F, 0, 512 * i + P * b:512 * i + P * b + P],
                                                    stage[:, i, F * b:F * b + F], ident[:, :])
                            last.then_inc(xt_ps_done, 1)
                        for i in range(2):
                            g = 2 * g2 + i
                            wait_alone(pe, xt_done, PRIME + NG * n + g + 1)
                            wait_alone(pe, ht_done, NG * n + g + 1)
                            pe.matmul(z_ps[0:F, 1, 512 * i:512 * i + 512], wgt[:, l, :], xt_sb[:, i, :],
                                      start=True, stop=True).then_inc(ht_ps_done, 1)
                        for i in range(2):
                            g = 2 * g2 + i
                            wait_alone(pe, ht_done, PRIME + NG * n + g + 1)
                            wait_alone(pe, proj_done, NG * n + g + 1)
                            for b in range(GB):
                                last = pe.matmul(acc_ps[:, i, (F + 2) * b:(F + 2) * (b + 1)],
                                                 ht_sb[:, i, P * b:P * b + P], proj[:, l, :], start=True, stop=True)
                            last.then_inc(proj_ps_done, 1)
                pe.wait_ge(abs_done, L + 1)
                pe.wait_ge(prep_rows_done, 2 * NP * L)
                pe.transpose(col_ps[0:1, 0:P], t_abs[:, :], ident[:, :]).then_inc(abs_t_done, 1)
                pe.wait_ge(top_done, L + 1)
                pe.matmul(col_ps[:, 256:257], ones[0:1, :], t_top[:, 1:2], start=True, stop=True)\
                  .then_inc(scale_ps_done, 1)
                with pe.Fori(0, NG // 2) as g2:
                    for i in range(2):
                        g = 2 * g2 + i
                        pe.wait_ge(diag_done, NG * L + g + 1)
                        pe.wait_ge(trow_done, NG * L + g + 1)
                        pe.matmul(z_ps[:, 0, 512 * i:512 * i + 512], ones[:, :],
                                  t_diag[:, i, :, :].rearrange("p b n -> p (b n)"), start=True, stop=True)\
                          .then_inc(trow_ps_done, 1)
                clear([acc_ps[:, 0, 0:FA]], FA)
                with pe.Fori(0, NB - 1) as b:
                    pe.matmul(acc_ps[:, 0, 0:FA], ones[:, :], h_aug[:, bass.ds(b, 1), :]
                              .rearrange("p a f -> p (a f)"), start=False, stop=False, skip_group_check=True)
                pe.matmul(acc_ps[:, 0, 0:FA], ones[:, :], h_aug[:, NB - 1, :], start=False, stop=True,
                          skip_group_check=True).then_inc(hsum_ps_done, 1)
                with pe.Fori(0, PQ) as pi:
                    prepare_rows(L, pi, 0)

                pe.wait_ge(prep_rows_done, 2 * (NP * L + PQ))
                pe.wait_ge(trow_done, PRIME + NG * (L + 1))
                pe.wait_ge(hsum_done, L + 1)
                mask_tile(L, 0, 0, True)
                mask_tile(L, 0, 1, False)
                clear([acc_ps[0:FA, i, :] for i in range(2)], 512)

                def body(q, row_max_on, prepare, finish, last, L=L):
                    for u in range(UN):
                        add_tile(L, q, u)
                        if prepare and u == 8:
                            prepare_rows(L, q + PQ, q // PQ)
                        ahead = u + PRIME
                        if ahead < UN:
                            mask_tile(L, q, ahead, ahead % SB == 0)
                        elif not last:
                            if prepare and ahead == UN:
                                pe.wait_ge(prep_rows_done, 2 * (NP * L + PQ + 1 + q))
                            mask_tile(L, q + 1, ahead - UN, ahead == UN)

                def close(s, L=L):
                    pe.wait_ge(acc_t_done, 2 * (NS * L) + 2 * (s + 1))
                    if not (isinstance(s, int) and s == NS - 1):
                        clear([acc_ps[0:FA, i, :] for i in range(2)], 512)
                    ready = PQ * (s + 2)
                    pe.wait_ge(prep_rows_done, 2 * (NP * L + (min(ready, NP) if isinstance(s, int) else ready)))
                    for i in range(2):
                        for b in range(SB // 2):
                            at = P * (SB // 2 * i + b)
                            last = pe.transpose(turned[i][:, FA * b:FA * b + FA], acc_t[:, at:at + P],
                                                ident[0:FA, 0:FA])
                        last.then_inc(turned_done, 1)

                layer_loop(pe, body, close, L)

            pe.wait_ge(parts_done, 1)
            pe.wait_ge(score_done, PRIME + 3 * KT)
            with pe.Fori(0, NS) as jc:
                pe.wait_ge(agg_done, 4 * jc)
                clear([z_flat[:, 512 * i:512 * i + 2 * XP] for i in range(4)], 2 * XP)
                with pe.Fori(0, NS // 2) as s2:
                    for i in range(2):
                        g = NS * jc + 2 * s2 + i
                        pe.wait_ge(adj_done, PRIME + g + 1)
                        pe.wait_ge(adj_done_a, PRIME + g + 1)
                        for b in range(SB):
                            for j in range(SB):
                                at = 512 * (j // 2) + XP * (j % 2)
                                last = pe.matmul(z_flat[:, at:at + XP], adj_b[:, i, b, P * j:P * j + P],
                                                 x_parts[:, bass.ds(SB * (2 * s2 + i) + b, 1), 0:XP]
                                                 .rearrange("p a n -> p (a n)"), start=False, stop=False,
                                                 skip_group_check=True)
                        last.then_inc(agg_step, 1)
                wait_alone(pe, agg_sum, jc + 1)
                for i in range(2):
                    for b in range(4):
                        last = pe.transpose(acc_ps[0:F, i, P * b:P * b + P], agg_sb[:, 4 * i + b, :], ident[:, :])
                    last.then_inc(aggt_ps_done, 1)
                pe.wait_ge(relu_done, jc)
                for i in range(2):
                    pe.wait_ge(aggt_done, 2 * jc + i + 1)
                    for b in range(4):
                        last = pe.matmul(col_ps[:, F * (4 * i + b):F * (4 * i + b + 1)],
                                         aggt_sb[:, i, P * b:P * b + P], ut[:, :], start=True, stop=True)
                last.then_inc(lin_ps_done, 1)


_INS = ['x', 'adj', 'L0_gnn_entity_embs', 'L0_gnn_W', 'L0_gnn_a', 'L1_gnn_W', 'L1_gnn_a', 'L2_gnn_W', 'L2_gnn_a',
        'L3_gnn_U']


def kernel(**inputs):
    import numpy as _np
    import concourse.bacc as _bacc
    from concourse import mybir as _mybir
    from concourse.bass_utils import run_bass_kernel_spmd as _run

    nc = _bacc.Bacc("TRN2", target_bir_lowering=False, num_devices=1)
    arrays, args = {}, []
    for name in _INS:
        a = _np.asarray(inputs[name])
        a = _np.ascontiguousarray(a.T if name == 'L3_gnn_U' else a)
        arrays[f"in_{name}"] = a
        args.append(nc.dram_tensor(f"in_{name}", a.shape, _mybir.dt.from_np(a.dtype), kind="ExternalInput").ap())
    shape = arrays["in_x"].shape
    args.append(nc.dram_tensor("out_x", shape, _mybir.dt.from_np(_np.dtype("float32")), kind="ExternalOutput").ap())
    build(nc, *args)
    r = _run(nc, [arrays], core_ids=[0])
    return r.results[0]["out_x"]
```

```python
from contextlib import ExitStack

import concourse.bass as bass
from concourse import mybir

ALU = mybir.AluOpType
ACT = mybir.ActivationFunctionType
AX_X = mybir.AxisListType.X
F32 = mybir.dt.float32
BF16 = mybir.dt.bfloat16
FP8 = mybir.dt.float8e4
I8 = mybir.dt.int8
I16 = mybir.dt.int16
I32 = mybir.dt.int32

P = 128
F = 64
FA = F + 1
SB = 8
PARTS = 3
MB = 112
BANK = 512
HB = 5
REST = BANK - (HB - 1) * MB
W = SB * P
UN = 16
NQ = 4
DEEP = 4
LAG = 3
GB = 4
NO_EDGE = -40
BIG = 2.0 ** 90
XP = PARTS * F + 1
TINY = 2.0 ** -100
EPS = 1e-5
SLOPES = (0.2, 0.2, 0.01)


def build(nc, x, adj, ent, W0, a0, W1, a1, W2, a2, UT, out):
    N = adj.shape[0]
    NB = N // P
    NS = N // W
    NP = NB // 2
    KT = NS * NB
    QW = N // NQ
    NG = NB // GB
    AHEAD = 5
    PQ = SB // 2
    fins3 = 3 * (NP - PQ + 1)
    CH_BASE = 3 * NS * NS // 2
    Ws, As = (W0, W1, W2), (a0, a1, a2)

    ctx = ExitStack()
    with ctx:
        def sb(name, shape, dt):
            return ctx.enter_context(nc.sbuf_tensor(name, shape, dt))

        def sem(name):
            return ctx.enter_context(nc.semaphore(name))

        mask_dram = nc.dram_tensor("mask_bytes", [N, N], I8, kind="Internal")
        mask_rows = mask_dram[:, :].rearrange("(r p) n -> r p n", p=P)
        banks = mask_dram[:, :].rearrange("(s k n) (c w) -> s c n k w", k=W // BANK, n=BANK, w=W)
        mask_full = banks[:, :, 0:BANK - REST, :, :].rearrange("s c (b p) k w -> s c p k b w", p=MB)
        mask_rest = banks[:, :, BANK - REST:BANK, :, :]
        mask_chunks = mask_dram[:, :].rearrange("(s b p) (c w) -> s c p b w", p=P, b=SB, w=W)
        adj_quarters = adj.rearrange("(r p) (c w) -> r c p w", p=P, w=QW)

        x_cur = sb("x_cur", [P, NB, F], F32)
        h_aug = sb("h_aug", [P, NB, FA], F32)
        t_row = sb("t_row", [P, N], F32)
        d_row = sb("d_row", [P, 2 * W], F32)
        s2_ring = sb("s2_ring", [PARTS, 2 * W], BF16)
        s2_mask = sb("s2_mask", [P, W], BF16)
        ints = sb("ints", [P, NQ, QW], I32)
        rowmask = sb("rowmask", [P, 2, N], I8)
        chunk = sb("chunk", [P, 2, 2 * HB, W], I8)
        score = sb("score", [P, DEEP, W], F32)
        prob = sb("prob", [P, DEEP, W], F32)
        scrap = sb("scrap", [P, QW], I8)
        ident = sb("ident", [P, P], F32)
        ident_b = sb("ident_b", [P, P], BF16)
        ones = sb("ones", [P, P], F32)
        zeros_b = sb("zeros_b", [P, 512], BF16)
        wgt = sb("wgt", [F, 3, F], F32)
        proj = sb("proj", [F, 3, F + 2], F32)
        ut = sb("ut", [F, F], F32)
        s_col = sb("s_col", [P, NB], F32)
        t_col = sb("t_col", [P, NB], F32)
        tn_col = sb("tn_col", [P, NB], F32)
        c_col = sb("c_col", [P, NB], F32)
        d_col = sb("d_col", [P, NB], F32)
        as_col = sb("as_col", [P, NB], F32)
        quarter_max = sb("quarter_max", [P, 2, NQ], F32)
        pair_max = sb("pair_max", [P, 2], F32)
        empty = sb("empty", [P, NB], F32)
        scale_col = sb("scale_col", [P, 1], F32)
        unscale = sb("unscale", [P, 1], F32)
        t_abs = sb("t_abs", [P, 1], F32)
        t_top = sb("t_top", [1, 2], F32)
        h_sum = sb("h_sum", [P, FA], F32)
        pr = sb("pr", [P, 12, 2], F32)
        s2_parts = sb("s2_parts", [P, 2, PARTS], BF16)
        d_diag = sb("d_diag", [P, 2, P], F32)
        h_tiles = sb("h_tiles", [P, 2, SB, FA], F32)
        acc_t = sb("acc_t", [FA, W], F32)
        acc_sb = sb("acc_sb", [P, SB, FA], F32)
        e_o = sb("e_o", [P, SB, F], F32)
        e_x = sb("e_x", [P, SB, F], F32)
        e_fill = sb("e_fill", [P, SB, FA], F32)
        e_small = sb("e_small", [P, 8, SB], F32)
        half = sb("half", [P, SB], F32)

        flat = score[:, :, :].rearrange("p a w -> p (a w)")
        stage = flat[:, 0:2 * GB * F].rearrange("p (i n) -> p i n", i=2)
        xt_sb = flat[0:F, 1024:2048].rearrange("p (i n) -> p i n", i=2)
        flat = prob[:, :, :].rearrange("p a w -> p (a w)")
        ht_sb = flat[0:F, 0:1024].rearrange("p (i n) -> p i n", i=2)
        t_diag = flat[:, 1024:2048].rearrange("p (i b n) -> p i b n", i=2, b=GB)

        x_parts = t_row[:, 0:NB * (XP + 1) // 2].bitcast(BF16).rearrange("p (b n) -> p b n", b=NB)
        adj_b = ints[:, :, :].rearrange("p i n -> p (i n)").bitcast(BF16).rearrange(
            "p (i b w) -> p i b w", i=2, b=SB)
        rest = h_aug[:, :, 0:F]
        acc3 = score[:, :, :].rearrange("p a w -> p (a w)")[:, 0:SB * XP].rearrange("p (b n) -> p b n", b=SB)
        agg_sb = prob[:, 0, 0:SB * F].rearrange("p (b n) -> p b n", b=SB)
        aggt_sb = prob[0:F, 1, :].rearrange("p (i n) -> p i n", i=2)

        z_ps = ctx.enter_context(nc.psum_tensor("z_ps", [P, 2, W], F32))
        acc_ps = ctx.enter_context(nc.psum_tensor("acc_ps", [P, 2, 512], F32))
        col_ps = ctx.enter_context(nc.psum_tensor("col_ps", [P, 512], F32))
        row_ps = ctx.enter_context(nc.psum_tensor("row_ps", [P, 512], F32))
        row_ps_b = row_ps[:, :].bitcast(BF16)
        edges8 = chunk[:, :, :, :].rearrange("p i b w -> p (i b w)").bitcast(FP8).rearrange(
            "p (i b w) -> p i b w", i=2, b=2 * HB)
        z_flat = z_ps[:, :, :].rearrange("p a w -> p (a w)")
        turned = [bank[:, 0:SB // 2 * FA] for bank in (col_ps, row_ps)]

        PRIME = 2
        inputs_in = sem("inputs_in")
        consts_done = sem("consts_done")
        ident_step = sem("ident_step")
        consts_cast = sem("consts_cast")
        ints_in = [sem(f"ints_in{c}") for c in range(NQ)]
        bytes_done = sem("bytes_done")
        stored = [sem(f"stored{i}") for i in range(2)]
        rows_in = [sem(f"rows_in{i}") for i in range(2)]
        chunk_in = [sem(f"chunk_in{i}") for i in range(2)]
        pair_done = sem("pair_done")
        max_done = sem("max_done")
        stage_done = sem("stage_done")
        xt_ps_done = sem("xt_ps_done")
        xt_done = sem("xt_done")
        ht_ps_done = sem("ht_ps_done")
        ht_done = sem("ht_done")
        proj_ps_done = sem("proj_ps_done")
        proj_done = sem("proj_done")
        dve_step = sem("dve_step")
        abs_done = sem("abs_done")
        abs_t_done = sem("abs_t_done")
        top_done = sem("top_done")
        scale_ps_done = sem("scale_ps_done")
        diag_done = sem("diag_done")
        trow_ps_done = sem("trow_ps_done")
        trow_done = sem("trow_done")
        cols_done = sem("cols_done")
        hsum_ps_done = sem("hsum_ps_done")
        hsum_done = sem("hsum_done")
        pool_step = sem("pool_step")
        prep_done = sem("prep_done")
        prep_ps_done = sem("prep_ps_done")
        prep_rows_done = sem("prep_rows_done")
        switched = sem("switched")
        mask_ps_done = sem("mask_ps_done")
        score_done = sem("score_done")
        exp_done = sem("exp_done")
        pv_done = sem("pv_done")
        acc_zero = sem("acc_zero")
        h_staged = sem("h_staged")
        acc_t_done = sem("acc_t_done")
        turned_done = sem("turned_done")
        acc_done = sem("acc_done")
        fixed = sem("fixed")
        recip_done = sem("recip_done")
        elu_in = sem("elu_in")
        elu_exp = sem("elu_exp")
        y_done = sem("y_done")
        sum_done = sem("sum_done")
        sq_done = sem("sq_done")
        var_done = sem("var_done")
        x_done = sem("x_done")
        parts_done = sem("parts_done")
        adj_done = sem("adj_done")
        adj_done_a = sem("adj_done_a")
        agg_step = sem("agg_step")
        agg_done = sem("agg_done")
        agg_sum = sem("agg_sum")
        aggt_ps_done = sem("aggt_ps_done")
        aggt_done = sem("aggt_done")
        lin_ps_done = sem("lin_ps_done")
        relu_done = sem("relu_done")
        out_in = sem("out_in")
        passed = {e.engine: sem(f"passed_{n}") for n, e in
                  (("sp", nc.sync), ("pool", nc.gpsimd), ("pe", nc.tensor), ("dve", nc.vector))}

        block = ctx.enter_context(nc.Block())

        def wait_alone(eng, which, value):
            eng.wait_ge(which, value)
            if not isinstance(value, int):
                eng.sem_inc(passed[eng.engine], 1)


        def layer_loop(eng, body, close, L):
            with eng.Fori(0, PQ - 1) as q:
                body(q, True, True, False, None, None)
            body(PQ - 1, True, True, False, None, 1)
            close(0)
            with eng.Fori(1, NS - 2) as s:
                body(PQ * s, True, True, True, s, None)
                with eng.Fori(1, PQ - 1) as r:
                    body(PQ * s + r, True, True, True, None, None)
                body(PQ * s + PQ - 1, True, True, True, None, s + 1)
                close(s)
            body(NP - 2 * PQ, True, True, True, NS - 2, None)
            with eng.Fori(NP - 2 * PQ + 1, NP - AHEAD) as q:
                body(q, True, True, True, None, None)
            body(NP - AHEAD, False, True, True, None, NS - 1)
            close(NS - 2)
            body(NP - PQ, False, False, True, NS - 1, None)
            with eng.Fori(NP - PQ + 1, NP - 1) as q:
                body(q, False, False, True, None, None)
            body(NP - 1, False, False, True, None, NS)
            close(NS - 1)

        def ends(closes):
            return isinstance(closes, int) and closes == NS

        PROJ = {0: (0, 1), 1: (2,), 2: (3,)}

        @block.sync
        def _(sp):
            sp.dma_start(h_aug[:, :, 0:F], ent.rearrange("(b p) f -> p b f", p=P)).then_inc(inputs_in, 16)
            sp.dma_start(x_cur[:, :, :], x.rearrange("(b p) f -> p b f", p=P)).then_inc(inputs_in, 16)
            for l in range(3):
                sp.dma_start(wgt[:, l, :], Ws[l]).then_inc(inputs_in, 16)
                sp.dma_start(proj[:, l, F:F + 1], As[l][0:F, :]).then_inc(inputs_in, 16)
                sp.dma_start(proj[:, l, F + 1:F + 2], As[l][F:2 * F, :]).then_inc(inputs_in, 16)
            sp.dma_start(ut[:, :], UT).then_inc(inputs_in, 16)

            def load_ints(r, c):
                wait_alone(sp, bytes_done, NQ * r + c + 1)
                sp.dma_start(ints[:, c, :], adj_quarters[bass.ds(r, 1), c, :, :].rearrange("a p w -> (a p) w"))\
                  .then_inc(ints_in[c], 16)

            def store_rows(r, i):
                wait_alone(sp, bytes_done, NQ + NQ * r + NQ)
                sp.dma_start(mask_rows[bass.ds(r, 1), :, :].rearrange("a p n -> (a p) n"), rowmask[:, i, :])\
                  .then_inc(stored[i], 16)

            def load_rows(L, r, i):
                wait_alone(sp, max_done, NB * NQ * L + NQ * r + NQ)
                sp.dma_start(rowmask[:, i, :], mask_rows[bass.ds(r, 1), :, :].rearrange("a p n -> (a p) n"))\
                  .then_inc(rows_in[i], 16)

            def load_chunk(L, g, i):
                blocks = chunk[:, i, :, :].rearrange("p (k b) w -> p k b w", b=HB)
                at = bass.ds(g // NS, 1), bass.ds(g % NS, 1)
                for half in range(W // BANK):
                    sp.dma_start(blocks[PARTS:PARTS + MB, half, 0:HB - 1, :],
                                 mask_full[at[0], at[1], :, half, :, :].rearrange("s c p b w -> (s c p) b w"))\
                      .then_inc(chunk_in[i], 16)
                sp.dma_start(blocks[PARTS:PARTS + REST, :, HB - 1, :], mask_rest[at[0], at[1], :, :, :]
                             .rearrange("s c p k w -> (s c p) k w")).then_inc(chunk_in[i], 16)

            for c in range(NQ):
                load_ints(0, c)
            with sp.Fori(0, AHEAD) as pair:
                for i in range(2):
                    for c in range(NQ):
                        load_ints(2 * pair + i + 1, c)
                    store_rows(2 * pair + i, i)

            def all_stored(upto):
                for i in range(2):
                    wait_alone(sp, stored[i], 16 * upto)

            for L in range(3):
                if L > 0:
                    load_rows(L, 0, 0)
                    with sp.Fori(0, AHEAD) as pair:
                        load_rows(L, 2 * pair + 1, 1)
                        load_rows(L, 2 * pair + 2, 0)
                    wait_alone(sp, mask_ps_done, KT * L)
                else:
                    all_stored(PQ)
                load_chunk(L, 0, 0)

                def body(q, row_max_on, prepare, finish, last):
                    for i in range(2):
                        g = 2 * q + i
                        if not (last and i == 1):
                            if L == 0:
                                all_stored(q + AHEAD if row_max_on else NP)
                            wait_alone(sp, mask_ps_done, KT * L + SB * g)
                            load_chunk(L, g + 1, (i + 1) % 2)
                        if row_max_on:
                            r = 2 * (q + AHEAD) + i
                            final = isinstance(q, int) and q == NP - AHEAD - 1 and i == 1
                            if L == 0:
                                if not final:
                                    for c in range(NQ):
                                        load_ints(r + 1, c)
                                store_rows(r, i)
                            elif not final:
                                load_rows(L, r + 1, (i + 1) % 2)

                with sp.Fori(0, NP - AHEAD - 1) as q:
                    body(q, True, True, True, False)
                body(NP - AHEAD - 1, True, True, True, False)
                with sp.Fori(NP - AHEAD, NP - 1) as q:
                    body(q, False, False, True, False)
                body(NP - 1, False, False, True, True)

            wait_alone(sp, mask_ps_done, KT * 3)
            with sp.Fori(0, NS) as jc:
                with sp.Fori(0, NS // 2) as s2:
                    for i in range(2):
                        g = NS * jc + 2 * s2 + i
                        wait_alone(sp, adj_done, g + 1)
                        wait_alone(sp, adj_done_a, g + 1)
                        sp.dma_start(chunk[:, i, 0:SB, :], mask_chunks[bass.ds(2 * s2 + i, 1), bass.ds(jc, 1), :, :, :]
                                     .rearrange("s c p b w -> (s c p) b w")).then_inc(chunk_in[i], 16)
            wait_alone(sp, x_done, fins3 + NS)
            sp.dma_start(out.rearrange("(b p) f -> p b f", p=P), x_cur[:, :, :]).then_inc(out_in, 16)
            sp.wait_ge(out_in, 16)

        @block.gpsimd
        def _(pool):
            pool.memset(ident[:, :], 0.0).then_inc(ident_step, 1)
            pool.memset(ones[:, :], 1.0).then_inc(consts_done, 1)
            pool.memset(zeros_b[:, :], 0.0).then_inc(consts_done, 1)
            pool.memset(half[:, :], -0.5).then_inc(consts_done, 1)
            pool.memset(h_aug[:, :, F:FA], 1.0).then_inc(consts_done, 1)
            pool.memset(d_diag[:, 0, :], 0.0).then_inc(ident_step, 1)
            pool.wait_ge(ident_step, 2)
            pool.affine_select(out=d_diag[:, 0, :], in_=d_diag[:, 0, :], compare_op=ALU.not_equal, fill=1.0,
                               base=-PARTS, pattern=[[-1, P]], channel_multiplier=1).then_inc(consts_done, 1)
            pool.affine_select(out=ident[:, :], in_=ident[:, :], compare_op=ALU.not_equal, fill=1.0, base=0,
                               pattern=[[-1, P]], channel_multiplier=1).then_inc(consts_done, 1)
            pool.wait_ge(inputs_in, 16 * 12)
            def stage_group(n, g, i, src):
                wait_alone(pool, xt_ps_done, NG * n + g + 1)
                pool.tensor_copy(stage[:, i, :].rearrange("p (b f) -> p b f", b=GB),
                                 src[:, bass.ds(GB * g, GB), 0:F]).then_inc(stage_done, 1)

            def prepare_pair(L, pi, steps):
                a = SLOPES[L]
                n = [0]

                def then(ins):
                    n[0] += 1
                    ins.then_inc(pool_step, 1)
                    wait_alone(pool, pool_step, steps + n[0])
                cols = bass.ds(2 * pi, 2)
                wait_alone(pool, pair_done, NP * L + pi + 1)
                none = pr[:, 11, :]
                (edge, m1, m2, y, up, low, m, s2, r1, r2) = (pr[:, k, :] for k in range(10))
                then(pool.tensor_scalar(none, pair_max[:, :], NO_EDGE / 2, None, ALU.is_lt))
                then(pool.tensor_copy(empty[:, cols], none))
                then(pool.tensor_scalar(edge, none, -1.0, 1.0, ALU.mult, ALU.add))
                then(pool.tensor_tensor(m1, pair_max[:, :], edge, ALU.mult))
                then(pool.tensor_scalar(m2, m1, scale_col[:, 0:1], None, ALU.mult))
                then(pool.tensor_tensor(y, m2, s_col[:, cols], ALU.add))
                then(pool.tensor_scalar(up, y, 0.0, 1.0 - a, ALU.max, ALU.mult))
                then(pool.tensor_scalar(low, y, a, None, ALU.mult))
                then(pool.tensor_tensor(m, up, low, ALU.add))
                then(pool.tensor_tensor(s2, as_col[:, cols], m, ALU.subtract))
                wait_alone(pool, prep_ps_done, NP * L + pi)
                then(pool.tensor_copy(s2_parts[:, :, 0], s2))
                then(pool.tensor_tensor(r1, s2, s2_parts[:, :, 0], ALU.subtract))
                then(pool.tensor_copy(s2_parts[:, :, 1], r1))
                then(pool.tensor_tensor(r2, r1, s2_parts[:, :, 1], ALU.subtract))
                then(pool.tensor_copy(s2_parts[:, :, 2], r2))
                then(pool.tensor_tensor(d_diag[:, :, :], ident[:, :].unsqueeze(1).to_broadcast([P, 2, P]),
                                        d_col[:, cols].unsqueeze(2).to_broadcast([P, 2, P]), ALU.mult))
                pool.tensor_copy(pr[:, 10, :], r2).then_inc(prep_done, 1)
                return n[0]

            def finish_rows(L, first, lo, nb, count, steps):
                n = [0]

                def then(ins):
                    n[0] += 1
                    ins.then_inc(pool_step, 1)
                    wait_alone(pool, pool_step, steps + n[0])
                rows, part = bass.ds(first, nb), bass.ds(lo, nb)
                acc, o, ex = acc_sb[:, part, :], e_o[:, 0:nb, :], e_x[:, 0:nb, :]
                fill = e_fill[:, 0:nb, :]
                rz, sm, mu, vs, v1, rs = (e_small[:, k, 0:nb] for k in range(6))

                def wide(col, w=F):
                    return col.unsqueeze(2).to_broadcast([P, nb, w])
                then(pool.tensor_tensor(fill, h_sum[:, :].unsqueeze(1).to_broadcast([P, nb, FA]),
                                        wide(empty[:, rows], FA), ALU.mult))
                then(pool.tensor_tensor(acc, acc, fill, ALU.add))
                pool.tensor_copy(e_small[:, 6, 0:nb], acc[:, :, F]).then_inc(fixed, 1)
                wait_alone(pool, recip_done, count + 1)
                then(pool.tensor_tensor(o, acc[:, :, 0:F], wide(rz), ALU.mult))
                if L == 0:
                    then(pool.tensor_tensor(o, o, x_cur[:, rows, :], ALU.add))
                pool.tensor_scalar(ex, o, 0.0, None, ALU.min).then_inc(elu_in, 1)
                then(pool.tensor_scalar(o, o, 0.0, -1.0, ALU.max, ALU.add))
                then(pool.tensor_tensor(o, o, x_cur[:, rows, :], ALU.add))
                wait_alone(pool, elu_exp, count + 1)
                pool.tensor_tensor(o, o, ex, ALU.add).then_inc(y_done, 1)
                normalise(then, rows, nb, count)
                return n[0]

            def normalise(then, rows, nb, count, extra=None):
                o, ex = e_o[:, 0:nb, :], e_x[:, 0:nb, :]
                rz, sm, mu, vs, v1, rs = (e_small[:, k, 0:nb] for k in range(6))

                def wide(col):
                    return col.unsqueeze(2).to_broadcast([P, nb, F])
                wait_alone(pool, sum_done, count + 1)
                then(pool.tensor_scalar(mu, sm, -1.0 / F, None, ALU.mult))
                if extra is not None:
                    then(pool.tensor_tensor(mu, mu, extra, ALU.add))
                then(pool.tensor_tensor(o, o, wide(mu), ALU.add))
                pool.tensor_tensor(ex, o, o, ALU.mult).then_inc(sq_done, 1)
                wait_alone(pool, var_done, count + 1)
                then(pool.tensor_scalar(v1, vs, 1.0 / F, EPS, ALU.mult, ALU.add))
                then(pool.tensor_tensor(rs, v1, half[:, 0:nb], ALU.pow))
                pool.tensor_tensor(x_cur[:, rows, :], o, wide(rs), ALU.mult).then_inc(x_done, 1)

            PREP = 16
            steps = 0
            for L in range(3):
                FIN_L = 2 + (2 if L == 0 else 1) + 2 + 2 + 2
                base = steps
                sources = (h_aug, x_cur) if L == 0 else (x_cur,)
                if L > 0:
                    wait_alone(pool, x_done, (NP - PQ + 1) * L)
                    wait_alone(pool, pv_done, DEEP + KT * L)
                for n, src in zip(PROJ[L], sources):
                    with pool.Fori(0, NG // 2) as g2:
                        for i in range(2):
                            stage_group(n, 2 * g2 + i, i, src)
                wait_alone(pool, cols_done, L + 1)
                with pool.Fori(0, PQ) as pi:
                    assert prepare_pair(L, pi, base + PREP * pi) == PREP
                base += PREP * PQ
                fins = (NP - PQ + 1) * L

                def body(q, row_max_on, prepare, finish, opens, closes, L=L, base=base, fins=fins):
                    if prepare:
                        if finish:
                            before = base + PREP * q + FIN_L * (q - PQ)
                        else:
                            before = base + PREP * q
                        prepare_pair(L, q + PQ, before)
                        before = before + PREP
                    else:
                        before = base + PREP * (NP - PQ) + FIN_L * (q - PQ)
                    if finish:
                        lo = 2 * (q % PQ)
                        wait_alone(pool, acc_done, 2 * (NS * L) + 2 * (q // PQ))
                        assert finish_rows(L, 2 * (q - PQ), lo, 2, fins + q - PQ, before) == FIN_L

                wait_alone(pool, hsum_done, L + 1)
                layer_loop(pool, body, lambda s: None, L)
                base += PREP * (NP - PQ) + FIN_L * (NP - PQ)
                wait_alone(pool, acc_done, 2 * NS * (L + 1))
                assert finish_rows(L, NB - SB, 0, SB, fins + NP - PQ, base) == FIN_L
                base += FIN_L
                steps = base

            fins = 3 * (NP - PQ + 1)
            AGG = 1
            FIN3 = 5
            with pool.Fori(0, NS) as jc:
                before = steps + (AGG + FIN3) * jc
                n = [0]

                def then(ins):
                    n[0] += 1
                    ins.then_inc(pool_step, 1)
                    wait_alone(pool, pool_step, before + n[0])
                wait_alone(pool, agg_done, 4 * jc + 4)
                then(pool.tensor_tensor(acc3[:, :, F:2 * F], acc3[:, :, F:2 * F], acc3[:, :, 2 * F:3 * F], ALU.add))
                pool.tensor_tensor(agg_sb, acc3[:, :, 0:F], acc3[:, :, F:2 * F], ALU.add).then_inc(agg_sum, 1)
                wait_alone(pool, relu_done, jc + 1)
                normalise(then, bass.ds(SB * jc, SB), SB, fins + jc, extra=e_small[:, 6, :])
                assert n[0] == AGG + FIN3

        @block.scalar
        def _(act):
            act.wait_ge(inputs_in, 16 * 12)
            act.sem_inc(bytes_done, NQ)
            act.sem_inc(exp_done, DEEP)
            act.sem_inc(ht_done, PRIME)
            act.sem_inc(trow_done, PRIME)

            def to_bytes(r, c, i):
                act.wait_ge(ints_in[c], 16 * (r + 1))
                act.wait_ge(max_done, NQ * r + c + 1)
                act.wait_ge(stored[i], 16 * (r // 2))
                act.activation(rowmask[:, i, c * QW:(c + 1) * QW], ints[:, c, :], ACT.Copy,
                               bias=float(NO_EDGE), scale=-float(NO_EDGE)).then_inc(bytes_done, 1)

            def copy_prepared(L, pi):
                act.wait_ge(prep_ps_done, NP * L + pi + 1)
                act.activation(d_row[:, bass.ds(2 * P * (pi % (2 * PQ)), 2 * P)], col_ps[:, 0:2 * P], ACT.Copy)\
                   .then_inc(prep_rows_done, 1)
                act.activation(s2_ring[0:PARTS, bass.ds(2 * P * (pi % (2 * PQ)), 2 * P)], row_ps_b[0:PARTS, 0:2 * P], ACT.Copy)\
                   .then_inc(prep_rows_done, 1)

            for L in range(3):
                for n in PROJ[L]:
                    with act.Fori(0, NG // 2) as g2:
                        for i in range(2):
                            g = 2 * g2 + i
                            act.wait_ge(ht_ps_done, PRIME + NG * n + g + 1)
                            act.wait_ge(proj_ps_done, NG * n + g + 1)
                            act.activation(ht_sb[:, i, :], z_ps[0:F, 1, 512 * i:512 * i + 512], ACT.Copy)\
                               .then_inc(ht_done, 1)
                with act.Fori(0, NG // 2) as g2:
                    for i in range(2):
                        g = 2 * g2 + i
                        act.wait_ge(trow_ps_done, PRIME + NG * L + g + 1)
                        act.activation(t_row[:, bass.ds(512 * g, 512)], z_ps[:, 0, 512 * i:512 * i + 512],
                                       ACT.Copy).then_inc(trow_done, 1)
                act.wait_ge(hsum_ps_done, L + 1)
                act.activation(h_sum[:, :], acc_ps[:, 0, 0:FA], ACT.Copy).then_inc(hsum_done, 1)
                if L == 0:
                    for i in range(2):
                        for c in range(NQ):
                            to_bytes(i, c, i)
                    with act.Fori(1, AHEAD) as pair:
                        for i in range(2):
                            for c in range(NQ):
                                to_bytes(2 * pair + i, c, i)
                        copy_prepared(L, pair - 1)
                else:
                    with act.Fori(0, PQ) as pi:
                        copy_prepared(L, pi)
                fins = (NP - PQ + 1) * L

                def stage_h(g, i):
                    act.activation(h_tiles[:, i, :, :], h_aug[:, bass.ds(SB * (g % NS), SB), :], ACT.Copy)\
                       .then_inc(h_staged, 1)

                act.wait_ge(pv_done, DEEP + KT * L)
                stage_h(0, 0)

                def elu(nb, count):
                    act.wait_ge(elu_in, count + 1)
                    act.activation(e_x[:, 0:nb, :], e_x[:, 0:nb, :], ACT.Exp).then_inc(elu_exp, 1)

                def body(q, row_max_on, prepare, finish, opens, closes, L=L, fins=fins):
                    convert = L == 0 and row_max_on
                    if convert:
                        to_bytes(2 * (q + AHEAD), 0, 0)
                    for u in range(UN):
                        k = UN * q + u
                        act.wait_ge(score_done, PRIME + KT * L + k + 1)
                        act.wait_ge(pv_done, KT * L + k + 1)
                        act.activation(prob[:, u % DEEP, :], score[:, u % DEEP, :], ACT.Exp,
                                       bias=t_col[:, bass.ds(k % NB, 1)]).then_inc(exp_done, 1)
                        if u == DEEP - 1:
                            stage_h(2 * q + 1, 1)
                        if u == SB + DEEP - 1 and not ends(closes):
                            stage_h(2 * q + 2, 0)
                        if opens is not None and u == 1:
                            copy_sums(opens - 1)
                        if opens is not None and u == 2:
                            copy_turned(opens - 1)
                        if convert and u % 2 and u < UN - 1:
                            i, c = (u + 2) // SB, (u + 2) % SB // 2
                            to_bytes(2 * (q + AHEAD) + i, c, i)
                        if prepare and u == 10:
                            copy_prepared(L, q + PQ)
                        if finish and u == 9:
                            elu(2, fins + q - PQ)

                def copy_sums(s, L=L):
                    act.wait_ge(pv_done, DEEP + KT * L + NB * (s + 1))
                    for i in range(2):
                        act.activation(acc_t[:, 512 * i:512 * i + 512], acc_ps[0:FA, i, :], ACT.Copy)\
                           .then_inc(acc_t_done, 1)

                def copy_turned(s, L=L, fins=fins):
                    act.wait_ge(x_done, fins + PQ * s)
                    for i in range(2):
                        act.wait_ge(turned_done, 2 * (NS * L + s) + i + 1)
                        act.activation(acc_sb[:, SB // 2 * i:SB // 2 * (i + 1), :],
                                       turned[i].rearrange("p (b f) -> p b f", b=SB // 2),
                                       ACT.Copy).then_inc(acc_done, 1)

                layer_loop(act, body, lambda s: None, L)
                copy_sums(NS - 1)
                copy_turned(NS - 1)
                elu(SB, fins + NP - PQ)

            act.sem_inc(adj_done_a, PRIME)
            with act.Fori(0, NS) as jc:
                with act.Fori(0, NS // 2) as s2:
                    for i in range(2):
                        g = NS * jc + 2 * s2 + i
                        act.wait_ge(chunk_in[i], 16 * (3 * CH_BASE + (NS // 2) * jc + s2 + 1))
                        act.wait_ge(agg_step, g + 1)
                        act.activation(adj_b[:, i, 0:SB // 2, :], chunk[:, i, 0:SB // 2, :], ACT.Relu, bias=1.0).then_inc(adj_done_a, 1)
                act.wait_ge(agg_step, PRIME + NS * jc + NS)
                act.wait_ge(x_done, fins3 + jc)
                for i in range(4):
                    act.activation(acc3[:, 2 * i:2 * i + 2, :],
                                   z_flat[:, 512 * i:512 * i + 2 * XP].rearrange("p (b n) -> p b n", b=2),
                                   ACT.Copy).then_inc(agg_done, 1)
                for i in range(2):
                    act.wait_ge(aggt_ps_done, 2 * jc + i + 1)
                    act.activation(aggt_sb[:, i, :], acc_ps[0:F, i, :], ACT.Copy).then_inc(aggt_done, 1)

        @block.vector
        def _(dve):
            dve.sem_inc(max_done, 2 * NQ)
            dve.sem_inc(xt_done, PRIME)
            dve.sem_inc(proj_done, PRIME)
            dve.sem_inc(score_done, PRIME)
            dve.memset(chunk[0:PARTS, :, :, :].rearrange("p i b w -> p (i b w)").bitcast(I16), 0x3838)\
               .then_inc(consts_cast, 1)
            dve.wait_ge(consts_done, 6)
            dve.wait_ge(inputs_in, 16 * 12)
            dve.tensor_copy(ident_b[:, :], ident[:, :]).then_inc(consts_cast, 1)
            for half in range(W // BANK):
                for b in range(HB):
                    at = BANK * half + MB * b
                    width = min(MB, BANK * (half + 1) - at)
                    dve.tensor_scalar(s2_mask[:, at:at + width], d_diag[:, 0, 0:width], BIG, None, ALU.mult)\
                       .then_inc(consts_cast, 1)
            for l in range(3):
                dve.tensor_copy(proj[:, l, 0:F], ident[0:F, 0:F]).then_inc(consts_cast, 1)
            steps = [0]

            def then(ins):
                steps[0] += 1
                ins.then_inc(dve_step, 1)
                dve.wait_ge(dve_step, steps[0])

            def row_max_quarter(L, r, c, i):
                if L == 0:
                    wait_alone(dve, bytes_done, NQ + NQ * r + c + 1)
                elif c == 0:
                    wait_alone(dve, rows_in[i], 16 * ((NB // 2) * (L - 1) + r // 2 + 1))
                wait_alone(dve, max_done, 2 * NQ + NB * NQ * L + NQ * r + c)
                start = quarter_max[:, i, c - 1:c] if c else -3.0e38
                dve.tensor_tensor_reduce(scrap[:, :], rowmask[:, i, c * QW:(c + 1) * QW],
                                         t_row[:, c * QW:(c + 1) * QW], 1.0, start, ALU.add, ALU.max,
                                         quarter_max[:, i, c:c + 1]).then_inc(max_done, 1)

            def pair_max_out(L, pair):
                dve.wait_ge(max_done, 2 * NQ + NB * NQ * L + 2 * NQ * (pair + 1))
                dve.wait_ge(prep_done, NP * L + pair)
                dve.tensor_copy(pair_max[:, :], quarter_max[:, :, NQ - 1]).then_inc(pair_done, 1)

            for L in range(3):
                a = SLOPES[L]
                if L > 0:
                    dve.wait_ge(pv_done, DEEP + KT * L)
                    dve.wait_ge(prep_done, NP * L)
                for n in PROJ[L]:
                    with dve.Fori(0, NG // 2) as g2:
                        for i in range(2):
                            g = 2 * g2 + i
                            dve.wait_ge(xt_ps_done, PRIME + NG * n + g + 1)
                            dve.wait_ge(ht_ps_done, NG * n + g + 1)
                            dve.tensor_copy(xt_sb[:, i, :], z_ps[0:F, 0, 512 * i:512 * i + 512]).then_inc(xt_done, 1)
                        for i in range(2):
                            g = 2 * g2 + i
                            rows = bass.ds(GB * g, GB)
                            dve.wait_ge(proj_ps_done, PRIME + NG * n + g + 1)
                            got = acc_ps[:, i, 0:GB * (F + 2)].rearrange("p (b f) -> p b f", b=GB)
                            if L > 0:
                                dve.tensor_copy(h_aug[:, rows, 0:F], got[:, :, 0:F])
                            if n != 0:
                                last = dve.tensor_copy(s_col[:, rows], got[:, :, F])
                            if n != 1:
                                last = dve.tensor_copy(t_col[:, rows], got[:, :, F + 1])
                            last.then_inc(proj_done, 1)
                dve.wait_ge(proj_done, PRIME + NG * (PROJ[L][-1] + 1))
                dve.tensor_scalar(d_col[:, :], s_col[:, :], 1.0 - a, None, ALU.mult)
                dve.tensor_scalar(as_col[:, :], s_col[:, :], a, None, ALU.mult)
                dve.tensor_scalar(c_col[:, :], t_col[:, :], a - 1.0, None, ALU.mult)
                dve.tensor_reduce(t_abs[:, :], t_col[:, :], AX_X, ALU.max, apply_absolute_value=True)\
                   .then_inc(abs_done, 1)
                dve.wait_ge(abs_t_done, L + 1)
                then(dve.tensor_reduce(t_top[:, 0:1], col_ps[0:1, 0:P], AX_X, ALU.max))
                then(dve.tensor_scalar(t_top[:, 0:1], t_top[:, 0:1], TINY, None, ALU.max))
                dve.tensor_scalar(t_top[:, 1:2].bitcast(I32), t_top[:, 0:1].bitcast(I32), 0x7F800000, None,
                                  ALU.bitwise_and).then_inc(top_done, 1)
                dve.wait_ge(scale_ps_done, L + 1)
                then(dve.tensor_copy(scale_col[:, :], col_ps[:, 256:257]))
                then(dve.reciprocal(unscale[:, :], scale_col[:, :]))
                then(dve.tensor_scalar(tn_col[:, :], t_col[:, :], unscale[:, 0:1], None, ALU.mult))
                dve.memset(e_small[:, 7, :], 0.0).then_inc(cols_done, 1)
                with dve.Fori(0, NG // 2) as g2:
                    for i in range(2):
                        g = 2 * g2 + i
                        dve.wait_ge(trow_ps_done, NG * L + g + 1)
                        dve.tensor_tensor(t_diag[:, i, :, :], ident[:, :].unsqueeze(1).to_broadcast([P, GB, P]),
                                          tn_col[:, bass.ds(GB * g, GB)].unsqueeze(2).to_broadcast([P, GB, P]),
                                          ALU.mult).then_inc(diag_done, 1)
                dve.wait_ge(trow_done, PRIME + NG * (L + 1))
                with dve.Fori(0, AHEAD) as pair:
                    for i in range(2):
                        for c in range(NQ):
                            row_max_quarter(L, 2 * pair + i, c, i)
                    pair_max_out(L, pair)
                fins = (NP - PQ + 1) * L

                def recip(nb, count):
                    dve.wait_ge(fixed, count + 1)
                    dve.reciprocal(e_small[:, 0, 0:nb], e_small[:, 6, 0:nb]).then_inc(recip_done, 1)

                def sums(nb, count):
                    dve.wait_ge(y_done, count + 1)
                    dve.tensor_reduce(e_small[:, 1, 0:nb], e_o[:, 0:nb, :], AX_X, ALU.add).then_inc(sum_done, 1)

                def squares(nb, count):
                    dve.wait_ge(sq_done, count + 1)
                    dve.tensor_reduce(e_small[:, 3, 0:nb], e_x[:, 0:nb, :], AX_X, ALU.add).then_inc(var_done, 1)

                def switch(s):
                    dve.tensor_copy(s2_mask[0:PARTS, :], s2_ring[:, bass.ds(W * (s % 2), W)]).then_inc(switched, 1)

                dve.wait_ge(prep_rows_done, 2 * (NP * L + PQ))
                switch(0)

                def body(q, row_max_on, prepare, finish, opens, closes, L=L, fins=fins):
                    for u in range(UN):
                        k = UN * q + u
                        dve.wait_ge(mask_ps_done, KT * L + k + 1)
                        dve.wait_ge(exp_done, KT * L + k + 1)
                        if closes is not None and not ends(closes) and u == UN - 1:
                            dve.wait_ge(prep_rows_done, 2 * (NP * L + PQ + 1 + q))
                            switch(closes)
                        dve.scalar_tensor_tensor(out=score[:, u % DEEP, :], in0=d_row[:, bass.ds(W * (q // PQ % 2), W)],
                                                 scalar=c_col[:, bass.ds(k % NB, 1)], in1=z_ps[:, u % 2, :],
                                                 op0=ALU.max, op1=ALU.add).then_inc(score_done, 1)
                        if row_max_on and u % 2:
                            i, c = u // SB, (u % SB) // 2
                            row_max_quarter(L, 2 * (q + AHEAD) + i, c, i)
                        if finish:
                            count = fins + q - PQ
                            if u == 7:
                                recip(2, count)
                            if u == 12:
                                sums(2, count)
                            if u == 15:
                                squares(2, count)
                    if row_max_on:
                        pair_max_out(L, q + AHEAD)

                layer_loop(dve, body, lambda s: None, L)
                recip(SB, fins + NP - PQ)
                sums(SB, fins + NP - PQ)
                squares(SB, fins + NP - PQ)

            dve.sem_inc(adj_done, PRIME)
            dve.wait_ge(x_done, fins3)
            dve.wait_ge(max_done, 2 * NQ + 3 * NB * NQ)
            parts = [x_parts[:, :, F * k:F * k + F] for k in range(PARTS)]
            then(dve.memset(x_parts[:, :, PARTS * F:XP], 1.0))
            then(dve.tensor_copy(parts[0], x_cur[:, :, :]))
            then(dve.tensor_tensor(rest, x_cur[:, :, :], parts[0], ALU.subtract))
            then(dve.tensor_copy(parts[1], rest))
            then(dve.tensor_tensor(rest, rest, parts[1], ALU.subtract))
            dve.tensor_copy(parts[2], rest).then_inc(parts_done, 1)
            base = steps[0]
            with dve.Fori(0, NS) as jc:
                with dve.Fori(0, NS // 2) as s2:
                    for i in range(2):
                        g = NS * jc + 2 * s2 + i
                        dve.wait_ge(chunk_in[i], 16 * (3 * CH_BASE + (NS // 2) * jc + s2 + 1))
                        dve.wait_ge(agg_step, g + 1)
                        dve.tensor_scalar(adj_b[:, i, SB // 2:SB, :], chunk[:, i, SB // 2:SB, :], 0.0, None,
                                          ALU.is_ge).then_inc(adj_done, 1)
                count = fins3 + jc
                dve.wait_ge(agg_done, 4 * jc + 4)
                dve.reciprocal(e_small[:, 0, :], acc3[:, :, PARTS * F]).then_inc(dve_step, 1)
                dve.wait_ge(dve_step, base + 2 * jc + 1)
                dve.tensor_scalar(e_small[:, 6, :], e_small[:, 0, :], 0.0, None, ALU.mult)
                dve.wait_ge(lin_ps_done, jc + 1)
                dve.tensor_tensor(e_o[:, :, :], col_ps[:, :].rearrange("p (b f) -> p b f", b=SB),
                                  e_small[:, 0, :].unsqueeze(2).to_broadcast([P, SB, F]), ALU.mult)\
                   .then_inc(dve_step, 1)
                dve.wait_ge(dve_step, base + 2 * jc + 2)
                dve.scalar_tensor_tensor(out=e_o[:, :, :], in0=e_o[:, :, :], scalar=0.0,
                                         in1=x_cur[:, bass.ds(SB * jc, SB), :], op0=ALU.max, op1=ALU.add)\
                   .then_inc(relu_done, 1)
                dve.wait_ge(relu_done, jc + 1)
                dve.tensor_reduce(e_small[:, 1, :], e_o[:, :, :], AX_X, ALU.add).then_inc(sum_done, 1)
                dve.wait_ge(sq_done, count + 1)
                dve.tensor_reduce(e_small[:, 3, :], e_x[:, :, :], AX_X, ALU.add).then_inc(var_done, 1)

        @block.tensor
        def _(pe):
            pe.sem_inc(xt_ps_done, PRIME)
            pe.sem_inc(ht_ps_done, PRIME)
            pe.sem_inc(proj_ps_done, PRIME)
            pe.sem_inc(trow_ps_done, PRIME)
            pe.sem_inc(pv_done, DEEP)
            pe.sem_inc(agg_step, PRIME)
            pe.wait_ge(consts_cast, 1 + 1 + W // BANK * HB + 3)

            def prepare_rows(L, pi, closed):
                pe.wait_ge(prep_done, NP * L + pi + 1)
                pe.wait_ge(prep_rows_done, 2 * (NP * L + pi))
                pe.wait_ge(acc_done, 2 * (NS * L + closed))
                pe.matmul(col_ps[:, 0:2 * P], ones[:, :], d_diag[:, :, :].rearrange("p b n -> p (b n)"),
                          start=True, stop=True)
                for b in range(2):
                    last = pe.transpose(row_ps_b[0:PARTS, P * b:P * b + P], s2_parts[:, b, :], ident_b[:, :])
                last.then_inc(prep_ps_done, 1)

            def mask_tile(L, q, u, first_of_chunk):
                k = UN * q + u
                if first_of_chunk:
                    wait_alone(pe, chunk_in[u // SB], 48 * ((NS * NS // 2) * L + q + 1))
                wait_alone(pe, score_done, KT * L + k + 1)
                for half in range(W // BANK):
                    for b in range(HB):
                        at = BANK * half + MB * b
                        width = min(MB, BANK * (half + 1) - at)
                        last = pe.matmul(z_ps[:, u % 2, at:at + width],
                                         edges8[0:PARTS + width, u // SB, HB * half + b, P * (u % SB):P * (u % SB) + P],
                                         s2_mask[0:PARTS + width, at:at + width], start=True, stop=True)
                last.then_inc(mask_ps_done, 1)

            def add_tile(L, q, u):
                k = UN * q + u
                if u % SB == 0:
                    wait_alone(pe, h_staged, NS * NS * L + 2 * q + u // SB + 1)
                pe.wait_ge(exp_done, DEEP + KT * L + k + 1)
                for i in range(2):
                    last = pe.matmul(acc_ps[0:FA, i, :], h_tiles[:, u // SB, u % SB, :],
                                     prob[:, u % DEEP, 512 * i:512 * i + 512], start=False, stop=False,
                                     skip_group_check=True)
                last.then_inc(pv_done, 1)

            def clear(banks, width):
                for bank in banks:
                    pe.matmul(bank, zeros_b[:, 0:bank.shape[0]], zeros_b[:, 0:width], start=True, stop=False,
                              skip_group_check=True)

            for L in range(3):
                for n in PROJ[L]:
                    l = L
                    with pe.Fori(0, NG // 2) as g2:
                        for i in range(2):
                            g = 2 * g2 + i
                            wait_alone(pe, stage_done, NG * n + g + 1)
                            wait_alone(pe, xt_done, NG * n + g + 1)
                            for b in range(GB):
                                last = pe.transpose(z_ps[0:F, 0, 512 * i + P * b:512 * i + P * b + P],
                                                    stage[:, i, F * b:F * b + F], ident[:, :])
                            last.then_inc(xt_ps_done, 1)
                        for i in range(2):
                            g = 2 * g2 + i
                            wait_alone(pe, xt_done, PRIME + NG * n + g + 1)
                            wait_alone(pe, ht_done, NG * n + g + 1)
                            pe.matmul(z_ps[0:F, 1, 512 * i:512 * i + 512], wgt[:, l, :], xt_sb[:, i, :],
                                      start=True, stop=True).then_inc(ht_ps_done, 1)
                        for i in range(2):
                            g = 2 * g2 + i
                            wait_alone(pe, ht_done, PRIME + NG * n + g + 1)
                            wait_alone(pe, proj_done, NG * n + g + 1)
                            for b in range(GB):
                                last = pe.matmul(acc_ps[:, i, (F + 2) * b:(F + 2) * (b + 1)],
                                                 ht_sb[:, i, P * b:P * b + P], proj[:, l, :], start=True, stop=True)
                            last.then_inc(proj_ps_done, 1)
                pe.wait_ge(abs_done, L + 1)
                pe.wait_ge(prep_rows_done, 2 * NP * L)
                pe.transpose(col_ps[0:1, 0:P], t_abs[:, :], ident[:, :]).then_inc(abs_t_done, 1)
                pe.wait_ge(top_done, L + 1)
                pe.matmul(col_ps[:, 256:257], ones[0:1, :], t_top[:, 1:2], start=True, stop=True)\
                  .then_inc(scale_ps_done, 1)
                with pe.Fori(0, NG // 2) as g2:
                    for i in range(2):
                        g = 2 * g2 + i
                        pe.wait_ge(diag_done, NG * L + g + 1)
                        pe.wait_ge(trow_done, NG * L + g + 1)
                        pe.matmul(z_ps[:, 0, 512 * i:512 * i + 512], ones[:, :],
                                  t_diag[:, i, :, :].rearrange("p b n -> p (b n)"), start=True, stop=True)\
                          .then_inc(trow_ps_done, 1)
                clear([acc_ps[:, 0, 0:FA]], FA)
                with pe.Fori(0, NB - 1) as b:
                    pe.matmul(acc_ps[:, 0, 0:FA], ones[:, :], h_aug[:, bass.ds(b, 1), :]
                              .rearrange("p a f -> p (a f)"), start=False, stop=False, skip_group_check=True)
                pe.matmul(acc_ps[:, 0, 0:FA], ones[:, :], h_aug[:, NB - 1, :], start=False, stop=True,
                          skip_group_check=True).then_inc(hsum_ps_done, 1)
                with pe.Fori(0, PQ) as pi:
                    prepare_rows(L, pi, 0)

                pe.wait_ge(switched, NS * L + 1)
                pe.wait_ge(trow_done, PRIME + NG * (L + 1))
                pe.wait_ge(hsum_done, L + 1)
                clear([acc_ps[0:FA, i, :] for i in range(2)], 512)
                for u in range(LAG):
                    mask_tile(L, 0, u, u == 0)

                def body(q, row_max_on, prepare, finish, opens, closes, L=L):
                    for u in range(UN):
                        add_tile(L, q, u)
                        if opens is not None and u == 1:
                            turn(opens - 1)
                        if prepare and u == 8:
                            prepare_rows(L, q + PQ, q // PQ)
                        ahead = u + LAG
                        if ahead < UN:
                            mask_tile(L, q, ahead, ahead % SB == 0)
                        elif not ends(closes):
                            if closes is not None and ahead == UN:
                                wait_alone(pe, switched, NS * L + closes + 1)
                            mask_tile(L, q + 1, ahead - UN, ahead == UN)

                def close(s, L=L):
                    pe.wait_ge(acc_t_done, 2 * (NS * L) + 2 * (s + 1))
                    if not (isinstance(s, int) and s == NS - 1):
                        clear([acc_ps[0:FA, i, :] for i in range(2)], 512)

                def turn(s, L=L):
                    ready = PQ * (s + 2)
                    pe.wait_ge(prep_rows_done, 2 * (NP * L + (min(ready, NP) if isinstance(s, int) else ready)))
                    for i in range(2):
                        for b in range(SB // 2):
                            at = P * (SB // 2 * i + b)
                            last = pe.transpose(turned[i][:, FA * b:FA * b + FA], acc_t[:, at:at + P],
                                                ident[0:FA, 0:FA])
                        last.then_inc(turned_done, 1)

                layer_loop(pe, body, close, L)
                turn(NS - 1)

            pe.wait_ge(parts_done, 1)
            pe.wait_ge(score_done, PRIME + 3 * KT)
            with pe.Fori(0, NS) as jc:
                pe.wait_ge(agg_done, 4 * jc)
                clear([z_flat[:, 512 * i:512 * i + 2 * XP] for i in range(4)], 2 * XP)
                with pe.Fori(0, NS // 2) as s2:
                    for i in range(2):
                        g = NS * jc + 2 * s2 + i
                        pe.wait_ge(adj_done, PRIME + g + 1)
                        pe.wait_ge(adj_done_a, PRIME + g + 1)
                        for b in range(SB):
                            for j in range(SB):
                                at = 512 * (j // 2) + XP * (j % 2)
                                last = pe.matmul(z_flat[:, at:at + XP], adj_b[:, i, b, P * j:P * j + P],
                                                 x_parts[:, bass.ds(SB * (2 * s2 + i) + b, 1), 0:XP]
                                                 .rearrange("p a n -> p (a n)"), start=False, stop=False,
                                                 skip_group_check=True)
                        last.then_inc(agg_step, 1)
                wait_alone(pe, agg_sum, jc + 1)
                for i in range(2):
                    for b in range(4):
                        last = pe.transpose(acc_ps[0:F, i, P * b:P * b + P], agg_sb[:, 4 * i + b, :], ident[:, :])
                    last.then_inc(aggt_ps_done, 1)
                pe.wait_ge(relu_done, jc)
                for i in range(2):
                    pe.wait_ge(aggt_done, 2 * jc + i + 1)
                    for b in range(4):
                        last = pe.matmul(col_ps[:, F * (4 * i + b):F * (4 * i + b + 1)],
                                         aggt_sb[:, i, P * b:P * b + P], ut[:, :], start=True, stop=True)
                last.then_inc(lin_ps_done, 1)


_INS = ['x', 'adj', 'L0_gnn_entity_embs', 'L0_gnn_W', 'L0_gnn_a', 'L1_gnn_W', 'L1_gnn_a', 'L2_gnn_W', 'L2_gnn_a',
        'L3_gnn_U']


def kernel(**inputs):
    import numpy as _np
    import concourse.bacc as _bacc
    from concourse import mybir as _mybir
    from concourse.bass_utils import run_bass_kernel_spmd as _run

    nc = _bacc.Bacc("TRN2", target_bir_lowering=False, num_devices=1)
    arrays, args = {}, []
    for name in _INS:
        a = _np.asarray(inputs[name])
        a = _np.ascontiguousarray(a.T if name == 'L3_gnn_U' else a)
        arrays[f"in_{name}"] = a
        args.append(nc.dram_tensor(f"in_{name}", a.shape, _mybir.dt.from_np(a.dtype), kind="ExternalInput").ap())
    shape = arrays["in_x"].shape
    args.append(nc.dram_tensor("out_x", shape, _mybir.dt.from_np(_np.dtype("float32")), kind="ExternalOutput").ap())
    build(nc, *args)
    r = _run(nc, [arrays], core_ids=[0])
    return r.results[0]["out_x"]
```

```python
from contextlib import ExitStack

import concourse.bass as bass
from concourse import mybir

ALU = mybir.AluOpType
ACT = mybir.ActivationFunctionType
AX_X = mybir.AxisListType.X
F32 = mybir.dt.float32
BF16 = mybir.dt.bfloat16
FP8 = mybir.dt.float8e4
I8 = mybir.dt.int8
I16 = mybir.dt.int16
I32 = mybir.dt.int32

P = 128
F = 64
FA = F + 1
SB = 8
PARTS = 3
MB = 112
BANK = 512
HB = 5
REST = BANK - (HB - 1) * MB
W = SB * P
UN = 16
NQ = 4
DEEP = 4
LAG = 3
GB = 4
PD = 4
NO_EDGE = -40
BIG = 2.0 ** 90
XP = PARTS * F + 1
TINY = 2.0 ** -100
EPS = 1e-5
SLOPES = (0.2, 0.2, 0.01)


def build(nc, x, adj, ent, W0, a0, W1, a1, W2, a2, UT, out):
    N = adj.shape[0]
    NB = N // P
    NS = N // W
    NP = NB // 2
    KT = NS * NB
    QW = N // NQ
    NG = NB // GB
    AHEAD = 5
    PQ = SB // 2
    fins3 = 3 * (NP - PQ + 1)
    EARLY = NB - 2 * SB
    PART_OPS = 5
    CH_BASE = 3 * NS * NS // 2
    Ws, As = (W0, W1, W2), (a0, a1, a2)

    ctx = ExitStack()
    with ctx:
        def sb(name, shape, dt):
            return ctx.enter_context(nc.sbuf_tensor(name, shape, dt))

        def sem(name):
            return ctx.enter_context(nc.semaphore(name))

        mask_dram = nc.dram_tensor("mask_bytes", [N, N], I8, kind="Internal")
        mask_rows = mask_dram[:, :].rearrange("(r p) n -> r p n", p=P)
        banks = mask_dram[:, :].rearrange("(s k n) (c w) -> s c n k w", k=W // BANK, n=BANK, w=W)
        mask_full = banks[:, :, 0:BANK - REST, :, :].rearrange("s c (b p) k w -> s c p k b w", p=MB)
        mask_rest = banks[:, :, BANK - REST:BANK, :, :]
        mask_chunks = mask_dram[:, :].rearrange("(s b p) (c w) -> s c p b w", p=P, b=SB, w=W)
        adj_quarters = adj.rearrange("(r p) (c w) -> r c p w", p=P, w=QW)

        x_cur = sb("x_cur", [P, NB, F], F32)
        h_aug = sb("h_aug", [P, NB, FA], F32)
        t_row = sb("t_row", [P, N], F32)
        d_row = sb("d_row", [P, 2 * W], F32)
        s2_ring = sb("s2_ring", [PARTS, 2 * W], BF16)
        s2_mask = sb("s2_mask", [P, W], BF16)
        ints = sb("ints", [P, NQ, QW], I32)
        rowmask = sb("rowmask", [P, 2, N], I8)
        chunk = sb("chunk", [P, 2, 2 * HB, W], I8)
        score = sb("score", [P, DEEP, W], F32)
        prob = sb("prob", [P, DEEP, W], F32)
        scrap = sb("scrap", [P, 2, QW], I8)
        ident = sb("ident", [P, P], F32)
        ident_b = sb("ident_b", [P, P], BF16)
        ones = sb("ones", [P, P], F32)
        zeros_b = sb("zeros_b", [P, 512], BF16)
        a_cols = sb("a_cols", [F, 3, 2], F32)
        wgt_t = sb("wgt_t", [F, 3, F], F32)
        proj = sb("proj", [F, 3, F + 2], F32)
        ut = sb("ut", [F, F], F32)
        s_col = sb("s_col", [P, NB], F32)
        t_col = sb("t_col", [P, NB], F32)
        tn_col = sb("tn_col", [P, NB], F32)
        c_col = sb("c_col", [P, NB], F32)
        d_col = sb("d_col", [P, NB], F32)
        as_col = sb("as_col", [P, NB], F32)
        quarter_max = sb("quarter_max", [P, 2, NQ], F32)
        pair_max = sb("pair_max", [P, 2], F32)
        empty = sb("empty", [P, NB], F32)
        scale_col = sb("scale_col", [P, 1], F32)
        unscale = sb("unscale", [P, 1], F32)
        t_abs = sb("t_abs", [P, 1], F32)
        t_top = sb("t_top", [1, 2], F32)
        h_sum = sb("h_sum", [P, FA], F32)
        pr = sb("pr", [P, 12, 2], F32)
        s2_parts = sb("s2_parts", [P, 2, PARTS], BF16)
        d_diag = sb("d_diag", [P, 2, P], F32)
        h_tiles = sb("h_tiles", [P, 2, SB, FA], F32)
        acc_t = sb("acc_t", [FA, W], F32)
        acc_sb = sb("acc_sb", [P, SB, FA], F32)
        e_o = sb("e_o", [P, SB, F], F32)
        e_x = sb("e_x", [P, SB, F], F32)
        e_fill = sb("e_fill", [P, SB, FA], F32)
        e_small = sb("e_small", [P, 8, SB], F32)
        half = sb("half", [P, SB], F32)

        flat = score[:, :, :].rearrange("p a w -> p (a w)")
        stage = flat[:, 0:PD * GB * F].rearrange("p (i n) -> p i n", i=PD)
        flat = prob[:, :, :].rearrange("p a w -> p (a w)")
        xt_sb = flat[0:F, 0:PD * GB * P].rearrange("p (i n) -> p i n", i=PD)
        t_diag = flat[:, PD * GB * P:2 * PD * GB * P].rearrange("p (i b n) -> p i b n", i=PD, b=GB)

        x_parts = t_row[:, 0:NB * (XP + 1) // 2].bitcast(BF16).rearrange("p (b n) -> p b n", b=NB)
        adj_b = ints[:, :, :].rearrange("p i n -> p (i n)").bitcast(BF16).rearrange(
            "p (i b w) -> p i b w", i=2, b=SB)
        rest = h_aug[:, :, 0:F]
        acc3 = score[:, :, :].rearrange("p a w -> p (a w)")[:, 0:SB * XP].rearrange("p (b n) -> p b n", b=SB)
        agg_sb = prob[:, 0, 0:SB * F].rearrange("p (b n) -> p b n", b=SB)
        aggt_sb = prob[0:F, 1, :].rearrange("p (i n) -> p i n", i=2)

        z_ps = ctx.enter_context(nc.psum_tensor("z_ps", [P, 2, W], F32))
        acc_ps = ctx.enter_context(nc.psum_tensor("acc_ps", [P, 2, 512], F32))
        col_ps = ctx.enter_context(nc.psum_tensor("col_ps", [P, 512], F32))
        row_ps = ctx.enter_context(nc.psum_tensor("row_ps", [P, 512], F32))
        row_ps_b = row_ps[:, :].bitcast(BF16)
        edges8 = chunk[:, :, :, :].rearrange("p i b w -> p (i b w)").bitcast(FP8).rearrange(
            "p (i b w) -> p i b w", i=2, b=2 * HB)
        z_flat = z_ps[:, :, :].rearrange("p a w -> p (a w)")
        xt_ps = z_flat.rearrange("p (i n) -> p i n", i=PD)
        proj_ps = [bank[:, 0:GB * (F + 2)] for bank in (acc_ps[:, 0, :], acc_ps[:, 1, :], col_ps, row_ps)]
        turned = [bank[:, 0:SB // 2 * FA] for bank in (col_ps, row_ps)]

        PRIME = 2
        inputs_in = sem("inputs_in")
        x_in = sem("x_in")
        consts_done = sem("consts_done")
        ident_step = sem("ident_step")
        consts_cast = sem("consts_cast")
        ints_in = [sem(f"ints_in{c}") for c in range(NQ)]
        bytes_done = sem("bytes_done")
        stored = [sem(f"stored{i}") for i in range(2)]
        rows_in = [sem(f"rows_in{i}") for i in range(2)]
        chunk_in = [sem(f"chunk_in{i}") for i in range(2)]
        pair_done = sem("pair_done")
        max_done = sem("max_done")
        stage_done = sem("stage_done")
        xt_ps_done = sem("xt_ps_done")
        xt_done = sem("xt_done")
        wt_ps_done = sem("wt_ps_done")
        wt_done = sem("wt_done")
        wa_ps_done = sem("wa_ps_done")
        proj_ps_done = sem("proj_ps_done")
        proj_done = sem("proj_done")
        dve_step = sem("dve_step")
        abs_done = sem("abs_done")
        abs_t_done = sem("abs_t_done")
        top_done = sem("top_done")
        scale_ps_done = sem("scale_ps_done")
        diag_done = sem("diag_done")
        trow_ps_done = sem("trow_ps_done")
        trow_done = sem("trow_done")
        cols_done = sem("cols_done")
        hsum_ps_done = sem("hsum_ps_done")
        hsum_done = sem("hsum_done")
        pool_step = sem("pool_step")
        prep_done = sem("prep_done")
        prep_ps_done = sem("prep_ps_done")
        prep_rows_done = sem("prep_rows_done")
        switched = sem("switched")
        mask_ps_done = sem("mask_ps_done")
        score_done = sem("score_done")
        exp_done = sem("exp_done")
        pv_done = sem("pv_done")
        acc_zero = sem("acc_zero")
        h_staged = sem("h_staged")
        acc_t_done = sem("acc_t_done")
        turned_done = sem("turned_done")
        acc_done = sem("acc_done")
        fixed = sem("fixed")
        recip_done = sem("recip_done")
        elu_in = sem("elu_in")
        elu_exp = sem("elu_exp")
        y_done = sem("y_done")
        sum_done = sem("sum_done")
        sq_done = sem("sq_done")
        var_done = sem("var_done")
        x_done = sem("x_done")
        parts_done = sem("parts_done")
        adj_done = sem("adj_done")
        adj_done_a = sem("adj_done_a")
        agg_step = sem("agg_step")
        agg_done = sem("agg_done")
        agg_sum = sem("agg_sum")
        aggt_ps_done = sem("aggt_ps_done")
        aggt_done = sem("aggt_done")
        lin_ps_done = sem("lin_ps_done")
        relu_done = sem("relu_done")
        out_in = sem("out_in")
        passed = {e.engine: sem(f"passed_{n}") for n, e in
                  (("sp", nc.sync), ("pool", nc.gpsimd), ("pe", nc.tensor), ("dve", nc.vector))}

        block = ctx.enter_context(nc.Block())

        def wait_alone(eng, which, value):
            eng.wait_ge(which, value)
            if not isinstance(value, int):
                eng.sem_inc(passed[eng.engine], 1)


        def layer_loop(eng, body, close, L):
            with eng.Fori(0, PQ - 1) as q:
                body(q, True, True, False, None, None)
            body(PQ - 1, True, True, False, None, 1)
            close(0)
            with eng.Fori(1, NS - 2) as s:
                body(PQ * s, True, True, True, s, None)
                with eng.Fori(1, PQ - 1) as r:
                    body(PQ * s + r, True, True, True, None, None)
                body(PQ * s + PQ - 1, True, True, True, None, s + 1)
                close(s)
            body(NP - 2 * PQ, True, True, True, NS - 2, None)
            with eng.Fori(NP - 2 * PQ + 1, NP - AHEAD) as q:
                body(q, True, True, True, None, None)
            body(NP - AHEAD, False, True, True, None, NS - 1)
            close(NS - 2)
            body(NP - PQ, False, False, True, NS - 1, None)
            with eng.Fori(NP - PQ + 1, NP - 1) as q:
                body(q, False, False, True, None, None)
            body(NP - 1, False, False, True, None, NS)
            close(NS - 1)

        def ends(closes):
            return isinstance(closes, int) and closes == NS

        def layer3_loop(eng, step, finish, beside=lambda g: None):
            for g in range(4):
                beside(g)
                step(0, g // 2, g % 2)
            with eng.Fori(2, NS // 2 - 1) as s2:
                for i in range(2):
                    step(0, s2, i)
            for i in range(2):
                step(0, NS // 2 - 1, i)
            with eng.Fori(1, NS) as jc:
                for k in range(4):
                    step(jc, k // 2, k % 2)
                    finish(jc - 1, k)
                with eng.Fori(2, NS // 2) as s2:
                    for i in range(2):
                        step(jc, s2, i)
            for k in range(4):
                finish(NS - 1, k)

        LAST_FIN = NP - PQ
        PROJ = {0: (0, 1), 1: (2,), 2: (3,)}

        @block.sync
        def _(sp):
            sp.dma_start(h_aug[:, :, 0:F], ent.rearrange("(b p) f -> p b f", p=P)).then_inc(inputs_in, 16)
            for l in range(3):
                sp.dma_start(proj[:, l, 0:F], Ws[l]).then_inc(inputs_in, 16)
                sp.dma_start(a_cols[:, l, 0:1], As[l][0:F, :]).then_inc(inputs_in, 16)
                sp.dma_start(a_cols[:, l, 1:2], As[l][F:2 * F, :]).then_inc(inputs_in, 16)
            sp.dma_start(ut[:, :], UT).then_inc(inputs_in, 16)
            sp.dma_start(x_cur[:, :, :], x.rearrange("(b p) f -> p b f", p=P)).then_inc(x_in, 16)

            def load_ints(r, c):
                wait_alone(sp, bytes_done, NQ * r + c + 1)
                sp.dma_start(ints[:, c, :], adj_quarters[bass.ds(r, 1), c, :, :].rearrange("a p w -> (a p) w"))\
                  .then_inc(ints_in[c], 16)

            def store_rows(r, i):
                wait_alone(sp, bytes_done, NQ + NQ * r + NQ)
                sp.dma_start(mask_rows[bass.ds(r, 1), :, :].rearrange("a p n -> (a p) n"), rowmask[:, i, :])\
                  .then_inc(stored[i], 16)

            def load_rows(L, r, i):
                wait_alone(sp, max_done, NB * NQ * L + NQ * r + NQ)
                sp.dma_start(rowmask[:, i, :], mask_rows[bass.ds(r, 1), :, :].rearrange("a p n -> (a p) n"))\
                  .then_inc(rows_in[i], 16)

            def load_chunk(L, g, i):
                blocks = chunk[:, i, :, :].rearrange("p (k b) w -> p k b w", b=HB)
                at = bass.ds(g // NS, 1), bass.ds(g % NS, 1)
                for half in range(W // BANK):
                    sp.dma_start(blocks[PARTS:PARTS + MB, half, 0:HB - 1, :],
                                 mask_full[at[0], at[1], :, half, :, :].rearrange("s c p b w -> (s c p) b w"))\
                      .then_inc(chunk_in[i], 16)
                sp.dma_start(blocks[PARTS:PARTS + REST, :, HB - 1, :], mask_rest[at[0], at[1], :, :, :]
                             .rearrange("s c p k w -> (s c p) k w")).then_inc(chunk_in[i], 16)

            for c in range(NQ):
                load_ints(0, c)
            with sp.Fori(0, AHEAD) as pair:
                for i in range(2):
                    for c in range(NQ):
                        load_ints(2 * pair + i + 1, c)
                    store_rows(2 * pair + i, i)

            def all_stored(upto):
                for i in range(2):
                    wait_alone(sp, stored[i], 16 * upto)

            for L in range(3):
                if L > 0:
                    load_rows(L, 0, 0)
                    with sp.Fori(0, AHEAD) as pair:
                        load_rows(L, 2 * pair + 1, 1)
                        load_rows(L, 2 * pair + 2, 0)
                    wait_alone(sp, mask_ps_done, KT * L)
                else:
                    all_stored(PQ)
                load_chunk(L, 0, 0)

                def body(q, row_max_on, prepare, finish, last):
                    for i in range(2):
                        g = 2 * q + i
                        if not (last and i == 1):
                            if L == 0:
                                all_stored(q + AHEAD if row_max_on else NP)
                            wait_alone(sp, mask_ps_done, KT * L + SB * g)
                            load_chunk(L, g + 1, (i + 1) % 2)
                        if row_max_on:
                            r = 2 * (q + AHEAD) + i
                            final = isinstance(q, int) and q == NP - AHEAD - 1 and i == 1
                            if L == 0:
                                if not final:
                                    for c in range(NQ):
                                        load_ints(r + 1, c)
                                store_rows(r, i)
                            elif not final:
                                load_rows(L, r + 1, (i + 1) % 2)

                with sp.Fori(0, NP - AHEAD - 1) as q:
                    body(q, True, True, True, False)
                body(NP - AHEAD - 1, True, True, True, False)
                with sp.Fori(NP - AHEAD, NP - 1) as q:
                    body(q, False, False, True, False)
                body(NP - 1, False, False, True, True)

            wait_alone(sp, mask_ps_done, KT * 3)
            with sp.Fori(0, NS) as jc:
                with sp.Fori(0, NS // 2) as s2:
                    for i in range(2):
                        g = NS * jc + 2 * s2 + i
                        wait_alone(sp, adj_done, g + 1)
                        wait_alone(sp, adj_done_a, g + 1)
                        sp.dma_start(chunk[:, i, 0:SB, :], mask_chunks[bass.ds(2 * s2 + i, 1), bass.ds(jc, 1), :, :, :]
                                     .rearrange("s c p b w -> (s c p) b w")).then_inc(chunk_in[i], 16)
            wait_alone(sp, x_done, fins3 + NS)
            sp.dma_start(out.rearrange("(b p) f -> p b f", p=P), x_cur[:, :, :]).then_inc(out_in, 16)
            sp.wait_ge(out_in, 16)

        @block.gpsimd
        def _(pool):
            pool.memset(ident[:, :], 0.0).then_inc(ident_step, 1)
            pool.memset(ones[:, :], 1.0).then_inc(consts_done, 1)
            pool.memset(zeros_b[:, :], 0.0).then_inc(consts_done, 1)
            pool.memset(half[:, :], -0.5).then_inc(consts_done, 1)
            pool.memset(h_aug[:, :, F:FA], 1.0).then_inc(consts_done, 1)
            pool.memset(d_diag[:, 0, :], 0.0).then_inc(ident_step, 1)
            pool.wait_ge(ident_step, 2)
            pool.affine_select(out=d_diag[:, 0, :], in_=d_diag[:, 0, :], compare_op=ALU.not_equal, fill=1.0,
                               base=-PARTS, pattern=[[-1, P]], channel_multiplier=1).then_inc(consts_done, 1)
            pool.affine_select(out=ident[:, :], in_=ident[:, :], compare_op=ALU.not_equal, fill=1.0, base=0,
                               pattern=[[-1, P]], channel_multiplier=1).then_inc(consts_done, 1)
            pool.wait_ge(inputs_in, 16 * 11)
            def prepare_pair(L, pi, steps):
                a = SLOPES[L]
                n = [0]

                def then(ins):
                    n[0] += 1
                    ins.then_inc(pool_step, 1)
                    wait_alone(pool, pool_step, steps + n[0])
                cols = bass.ds(2 * pi, 2)
                wait_alone(pool, pair_done, NP * L + pi + 1)
                none = pr[:, 11, :]
                (edge, m1, m2, y, up, low, m, s2, r1, r2) = (pr[:, k, :] for k in range(10))
                then(pool.tensor_scalar(none, pair_max[:, :], NO_EDGE / 2, None, ALU.is_lt))
                then(pool.tensor_copy(empty[:, cols], none))
                then(pool.tensor_scalar(edge, none, -1.0, 1.0, ALU.mult, ALU.add))
                then(pool.tensor_tensor(m1, pair_max[:, :], edge, ALU.mult))
                then(pool.tensor_scalar(m2, m1, scale_col[:, 0:1], None, ALU.mult))
                then(pool.tensor_tensor(y, m2, s_col[:, cols], ALU.add))
                then(pool.tensor_scalar(up, y, 0.0, 1.0 - a, ALU.max, ALU.mult))
                then(pool.tensor_scalar(low, y, a, None, ALU.mult))
                then(pool.tensor_tensor(m, up, low, ALU.add))
                then(pool.tensor_tensor(s2, as_col[:, cols], m, ALU.subtract))
                wait_alone(pool, prep_ps_done, NP * L + pi)
                then(pool.tensor_copy(s2_parts[:, :, 0], s2))
                then(pool.tensor_tensor(r1, s2, s2_parts[:, :, 0], ALU.subtract))
                then(pool.tensor_copy(s2_parts[:, :, 1], r1))
                then(pool.tensor_tensor(r2, r1, s2_parts[:, :, 1], ALU.subtract))
                then(pool.tensor_copy(s2_parts[:, :, 2], r2))
                then(pool.tensor_tensor(d_diag[:, :, :], ident[:, :].unsqueeze(1).to_broadcast([P, 2, P]),
                                        d_col[:, cols].unsqueeze(2).to_broadcast([P, 2, P]), ALU.mult))
                pool.tensor_copy(pr[:, 10, :], r2).then_inc(prep_done, 1)
                return n[0]

            def finish_rows(L, first, lo, nb, count, steps):
                n = [0]

                def then(ins):
                    n[0] += 1
                    ins.then_inc(pool_step, 1)
                    wait_alone(pool, pool_step, steps + n[0])
                rows, part = bass.ds(first, nb), bass.ds(lo, nb)
                acc, o, ex = acc_sb[:, part, :], e_o[:, 0:nb, :], e_x[:, 0:nb, :]
                fill = e_fill[:, 0:nb, :]
                rz, sm, mu, vs, v1, rs = (e_small[:, k, 0:nb] for k in range(6))

                def wide(col, w=F):
                    return col.unsqueeze(2).to_broadcast([P, nb, w])
                then(pool.tensor_tensor(fill, h_sum[:, :].unsqueeze(1).to_broadcast([P, nb, FA]),
                                        wide(empty[:, rows], FA), ALU.mult))
                then(pool.tensor_tensor(acc, acc, fill, ALU.add))
                pool.tensor_copy(e_small[:, 6, 0:nb], acc[:, :, F]).then_inc(fixed, 1)
                wait_alone(pool, recip_done, count + 1)
                then(pool.tensor_tensor(o, acc[:, :, 0:F], wide(rz), ALU.mult))
                if L == 0:
                    then(pool.tensor_tensor(o, o, x_cur[:, rows, :], ALU.add))
                pool.tensor_scalar(ex, o, 0.0, None, ALU.min).then_inc(elu_in, 1)
                then(pool.tensor_scalar(o, o, 0.0, -1.0, ALU.max, ALU.add))
                then(pool.tensor_tensor(o, o, x_cur[:, rows, :], ALU.add))
                wait_alone(pool, elu_exp, count + 1)
                pool.tensor_tensor(o, o, ex, ALU.add).then_inc(y_done, 1)
                normalise(then, rows, nb, count)
                return n[0]

            def normalise(then, rows, nb, count, extra=None):
                o, ex = e_o[:, 0:nb, :], e_x[:, 0:nb, :]
                rz, sm, mu, vs, v1, rs = (e_small[:, k, 0:nb] for k in range(6))

                def wide(col):
                    return col.unsqueeze(2).to_broadcast([P, nb, F])
                wait_alone(pool, sum_done, count + 1)
                then(pool.tensor_scalar(mu, sm, -1.0 / F, None, ALU.mult))
                if extra is not None:
                    then(pool.tensor_tensor(mu, mu, extra, ALU.add))
                then(pool.tensor_tensor(o, o, wide(mu), ALU.add))
                pool.tensor_tensor(ex, o, o, ALU.mult).then_inc(sq_done, 1)
                wait_alone(pool, var_done, count + 1)
                then(pool.tensor_scalar(v1, vs, 1.0 / F, EPS, ALU.mult, ALU.add))
                then(pool.tensor_tensor(rs, v1, half[:, 0:nb], ALU.pow))
                pool.tensor_tensor(x_cur[:, rows, :], o, wide(rs), ALU.mult).then_inc(x_done, 1)

            PREP = 16
            steps = 0
            for L in range(3):
                FIN_L = 2 + (2 if L == 0 else 1) + 2 + 2 + 2
                base = steps
                wait_alone(pool, cols_done, L + 1)
                with pool.Fori(0, PQ) as pi:
                    assert prepare_pair(L, pi, base + PREP * pi) == PREP
                base += PREP * PQ
                fins = (NP - PQ + 1) * L

                def body(q, row_max_on, prepare, finish, opens, closes, L=L, base=base, fins=fins):
                    if prepare:
                        if finish:
                            before = base + PREP * q + FIN_L * (q - PQ)
                        else:
                            before = base + PREP * q
                        prepare_pair(L, q + PQ, before)
                        before = before + PREP
                    else:
                        before = base + PREP * (NP - PQ) + FIN_L * (q - PQ)
                    if finish:
                        lo = 2 * (q % PQ)
                        wait_alone(pool, acc_done, 2 * (NS * L) + 2 * (q // PQ))
                        assert finish_rows(L, 2 * (q - PQ), lo, 2, fins + q - PQ, before) == FIN_L

                wait_alone(pool, hsum_done, L + 1)
                layer_loop(pool, body, lambda s: None, L)
                base += PREP * (NP - PQ) + FIN_L * (NP - PQ)
                wait_alone(pool, acc_done, 2 * NS * (L + 1))
                assert finish_rows(L, NB - SB, 0, SB, fins + NP - PQ, base) == FIN_L
                base += FIN_L
                steps = base

            fins = 3 * (NP - PQ + 1)
            AGG = 1
            FIN3 = 5
            with pool.Fori(0, NS) as jc:
                before = steps + (AGG + FIN3) * jc
                n = [0]

                def then(ins):
                    n[0] += 1
                    ins.then_inc(pool_step, 1)
                    wait_alone(pool, pool_step, before + n[0])
                wait_alone(pool, agg_done, 4 * jc + 4)
                then(pool.tensor_tensor(acc3[:, :, F:2 * F], acc3[:, :, F:2 * F], acc3[:, :, 2 * F:3 * F], ALU.add))
                pool.tensor_tensor(agg_sb, acc3[:, :, 0:F], acc3[:, :, F:2 * F], ALU.add).then_inc(agg_sum, 1)
                wait_alone(pool, relu_done, jc + 1)
                normalise(then, bass.ds(SB * jc, SB), SB, fins + jc, extra=e_small[:, 6, :])
                assert n[0] == AGG + FIN3

        @block.scalar
        def _(act):
            act.wait_ge(inputs_in, 16 * 11)
            act.sem_inc(bytes_done, NQ)
            act.sem_inc(exp_done, DEEP)
            act.sem_inc(adj_done_a, PRIME)
            act.sem_inc(xt_done, PD)
            act.sem_inc(trow_done, PD)

            def to_bytes(r, c, i):
                act.wait_ge(ints_in[c], 16 * (r + 1))
                act.wait_ge(max_done, NQ * r + c + 1)
                act.wait_ge(stored[i], 16 * (r // 2))
                act.activation(rowmask[:, i, c * QW:(c + 1) * QW], ints[:, c, :], ACT.Copy,
                               bias=float(NO_EDGE), scale=-float(NO_EDGE)).then_inc(bytes_done, 1)

            def copy_prepared(L, pi):
                act.wait_ge(prep_ps_done, NP * L + pi + 1)
                act.activation(d_row[:, bass.ds(2 * P * (pi % (2 * PQ)), 2 * P)], col_ps[:, 0:2 * P], ACT.Copy)\
                   .then_inc(prep_rows_done, 1)
                act.activation(s2_ring[0:PARTS, bass.ds(2 * P * (pi % (2 * PQ)), 2 * P)], row_ps_b[0:PARTS, 0:2 * P], ACT.Copy)\
                   .then_inc(prep_rows_done, 1)

            def elu(nb, count):
                act.wait_ge(elu_in, count + 1)
                act.activation(e_x[:, 0:nb, :], e_x[:, 0:nb, :], ACT.Exp).then_inc(elu_exp, 1)

            def project(n, g4, src):
                for i in range(PD):
                    g = PD * g4 + i
                    act.wait_ge(xt_ps_done, NG * n + g + 1)
                    act.activation(stage[:, i, :].rearrange("p (b f) -> p b f", b=GB),
                                   src[:, bass.ds(GB * g, GB), 0:F], ACT.Copy).then_inc(stage_done, 1)
                for i in range(PD):
                    g = PD * g4 + i
                    act.wait_ge(xt_ps_done, PD + NG * n + g + 1)
                    act.wait_ge(proj_ps_done, NG * n + g + 1)
                    act.activation(xt_sb[:, i, :], xt_ps[0:F, i, :], ACT.Copy).then_inc(xt_done, 1)

            for L in range(3):
                if L == 0:
                    for n, src in zip(PROJ[L], (h_aug, x_cur)):
                        if n == 1:
                            act.wait_ge(x_in, 16)
                        for g4 in range(NG // PD):
                            project(n, g4, src)
                            to_bytes(n, g4, n)
                else:
                    n, = PROJ[L]
                    fins = (NP - PQ + 1) * (L - 1)
                    act.wait_ge(x_done, fins + LAST_FIN)
                    project(n, 0, x_cur)
                    elu(SB, fins + LAST_FIN)
                    with act.Fori(1, NG // PD - 1) as g4:
                        project(n, g4, x_cur)
                    act.wait_ge(x_done, fins + LAST_FIN + 1)
                    project(n, NG // PD - 1, x_cur)
                with act.Fori(0, NG // PD) as g4:
                    for i in range(PD):
                        g = PD * g4 + i
                        act.wait_ge(trow_ps_done, PD + NG * L + g + 1)
                        act.activation(t_row[:, bass.ds(GB * P * g, GB * P)], xt_ps[:, i, :], ACT.Copy)\
                           .then_inc(trow_done, 1)
                act.wait_ge(hsum_ps_done, L + 1)
                act.activation(h_sum[:, :], acc_ps[:, 0, 0:FA], ACT.Copy).then_inc(hsum_done, 1)
                if L == 0:
                    with act.Fori(1, AHEAD) as pair:
                        for i in range(2):
                            for c in range(NQ):
                                to_bytes(2 * pair + i, c, i)
                        copy_prepared(L, pair - 1)
                else:
                    with act.Fori(0, PQ) as pi:
                        copy_prepared(L, pi)
                fins = (NP - PQ + 1) * L

                def stage_h(g, i):
                    act.activation(h_tiles[:, i, :, :], h_aug[:, bass.ds(SB * (g % NS), SB), :], ACT.Copy)\
                       .then_inc(h_staged, 1)

                act.wait_ge(pv_done, DEEP + KT * L)
                stage_h(0, 0)

                def body(q, row_max_on, prepare, finish, opens, closes, L=L, fins=fins):
                    convert = L == 0 and row_max_on
                    if convert:
                        to_bytes(2 * (q + AHEAD), 0, 0)
                    for u in range(UN):
                        k = UN * q + u
                        act.wait_ge(score_done, PRIME + KT * L + k + 1)
                        act.wait_ge(pv_done, KT * L + k + 1)
                        act.activation(prob[:, u % DEEP, :], score[:, u % DEEP, :], ACT.Exp,
                                       bias=t_col[:, bass.ds(k % NB, 1)]).then_inc(exp_done, 1)
                        if u == DEEP - 1:
                            stage_h(2 * q + 1, 1)
                        if u == SB + DEEP - 1 and not ends(closes):
                            stage_h(2 * q + 2, 0)
                        if opens is not None and u == 1:
                            copy_sums(opens - 1)
                        if opens is not None and u == 2:
                            copy_turned(opens - 1)
                        if convert and u % 2 and u < UN - 1:
                            i, c = (u + 2) // SB, (u + 2) % SB // 2
                            to_bytes(2 * (q + AHEAD) + i, c, i)
                        if prepare and u == 10:
                            copy_prepared(L, q + PQ)
                        if finish and u == 9:
                            elu(2, fins + q - PQ)

                def copy_sums(s, L=L):
                    act.wait_ge(pv_done, DEEP + KT * L + NB * (s + 1))
                    for i in range(2):
                        act.activation(acc_t[:, 512 * i:512 * i + 512], acc_ps[0:FA, i, :], ACT.Copy)\
                           .then_inc(acc_t_done, 1)

                def copy_turned(s, L=L, fins=fins):
                    act.wait_ge(x_done, fins + PQ * s)
                    for i in range(2):
                        act.wait_ge(turned_done, 2 * (NS * L + s) + i + 1)
                        act.activation(acc_sb[:, SB // 2 * i:SB // 2 * (i + 1), :],
                                       turned[i].rearrange("p (b f) -> p b f", b=SB // 2),
                                       ACT.Copy).then_inc(acc_done, 1)

                layer_loop(act, body, lambda s: None, L)
                copy_sums(NS - 1)
                copy_turned(NS - 1)

            def to_bf16(jc, s2, i):
                g = NS * jc + 2 * s2 + i
                act.wait_ge(chunk_in[i], 16 * (3 * CH_BASE + (NS // 2) * jc + s2 + 1))
                act.wait_ge(agg_step, g + 1)
                act.activation(adj_b[:, i, 0:SB // 2, :], chunk[:, i, 0:SB // 2, :], ACT.Relu, bias=1.0)\
                   .then_inc(adj_done_a, 1)

            def copy_columns(jc, k):
                if k == 0:
                    act.wait_ge(agg_step, PRIME + NS * jc + NS)
                    act.wait_ge(x_done, fins3 + jc)
                    for i in range(4):
                        act.activation(acc3[:, 2 * i:2 * i + 2, :],
                                       z_flat[:, 512 * i:512 * i + 2 * XP].rearrange("p (b n) -> p b n", b=2),
                                       ACT.Copy).then_inc(agg_done, 1)
                if k == 1:
                    for i in range(2):
                        act.wait_ge(aggt_ps_done, 2 * jc + i + 1)
                        act.activation(aggt_sb[:, i, :], acc_ps[0:F, i, :], ACT.Copy).then_inc(aggt_done, 1)

            def beside(g):
                if g == 1:
                    elu(SB, 2 * (NP - PQ + 1) + LAST_FIN)

            layer3_loop(act, to_bf16, copy_columns, beside)

        @block.vector
        def _(dve):
            dve.sem_inc(max_done, 2 * NQ)
            dve.sem_inc(adj_done, PRIME)
            dve.sem_inc(proj_done, PD)
            dve.sem_inc(score_done, PRIME)
            dve.memset(chunk[0:PARTS, :, :, :].rearrange("p i b w -> p (i b w)").bitcast(I16), 0x3838)\
               .then_inc(consts_cast, 1)
            dve.wait_ge(consts_done, 6)
            dve.wait_ge(inputs_in, 16 * 11)
            dve.tensor_copy(ident_b[:, :], ident[:, :]).then_inc(consts_cast, 1)
            for half in range(W // BANK):
                for b in range(HB):
                    at = BANK * half + MB * b
                    width = min(MB, BANK * (half + 1) - at)
                    dve.tensor_scalar(s2_mask[:, at:at + width], d_diag[:, 0, 0:width], BIG, None, ALU.mult)\
                       .then_inc(consts_cast, 1)
            dve.wait_ge(wt_ps_done, 1)
            dve.tensor_copy(wgt_t[:, :, :], col_ps[0:F, 0:3 * F].rearrange("p (l f) -> p l f", l=3)).then_inc(wt_done, 1)
            dve.wait_ge(wa_ps_done, 1)
            dve.tensor_copy(proj[:, :, F:F + 2], row_ps[0:F, 0:6].rearrange("p (l f) -> p l f", l=3))\
               .then_inc(consts_cast, 1)
            steps = [0]

            def then(ins):
                steps[0] += 1
                ins.then_inc(dve_step, 1)
                dve.wait_ge(dve_step, steps[0])

            def row_max_quarter(L, r, c, i):
                if L == 0:
                    wait_alone(dve, bytes_done, NQ + NQ * r + c + 1)
                elif c == 0:
                    wait_alone(dve, rows_in[i], 16 * ((NB // 2) * (L - 1) + r // 2 + 1))
                wait_alone(dve, max_done, 2 * NQ + NB * NQ * L + NQ * r + c - 1)
                dve.tensor_tensor_reduce(scrap[:, c % 2, :], rowmask[:, i, c * QW:(c + 1) * QW],
                                         t_row[:, c * QW:(c + 1) * QW], 1.0, -3.0e38, ALU.add, ALU.max,
                                         quarter_max[:, i, c:c + 1]).then_inc(max_done, 1)

            def pair_max_out(L, pair):
                dve.wait_ge(max_done, 2 * NQ + NB * NQ * L + 2 * NQ * (pair + 1))
                dve.wait_ge(prep_done, NP * L + pair)
                dve.tensor_reduce(pair_max[:, :], quarter_max[:, :, :], AX_X, ALU.max).then_inc(pair_done, 1)
                wait_alone(dve, pair_done, NP * L + pair + 1)

            def recip(nb, count):
                dve.wait_ge(fixed, count + 1)
                dve.reciprocal(e_small[:, 0, 0:nb], e_small[:, 6, 0:nb]).then_inc(recip_done, 1)

            def sums(nb, count):
                dve.wait_ge(y_done, count + 1)
                dve.tensor_reduce(e_small[:, 1, 0:nb], e_o[:, 0:nb, :], AX_X, ALU.add).then_inc(sum_done, 1)

            def squares(nb, count):
                dve.wait_ge(sq_done, count + 1)
                dve.tensor_reduce(e_small[:, 3, 0:nb], e_x[:, 0:nb, :], AX_X, ALU.add).then_inc(var_done, 1)

            def take_projected(L, n, g4):
                for i in range(PD):
                    g = PD * g4 + i
                    rows = bass.ds(GB * g, GB)
                    dve.wait_ge(proj_ps_done, PD + NG * n + g + 1)
                    got = proj_ps[i].rearrange("p (b f) -> p b f", b=GB)
                    if L > 0:
                        dve.tensor_copy(h_aug[:, rows, 0:F], got[:, :, 0:F])
                    if n != 0:
                        last = dve.tensor_copy(s_col[:, rows], got[:, :, F])
                    if n != 1:
                        last = dve.tensor_copy(t_col[:, rows], got[:, :, F + 1])
                    last.then_inc(proj_done, 1)

            parts = [x_parts[:, :, F * k:F * k + F] for k in range(PARTS)]

            def part_step(k, lo, hi):
                x, left, part = x_cur[:, lo:hi, :], rest[:, lo:hi, :], [p[:, lo:hi, :] for p in parts]
                if k == 0:
                    then(dve.tensor_copy(part[0], x))
                if k == 1:
                    then(dve.tensor_tensor(left, x, part[0], ALU.subtract))
                if k == 2:
                    then(dve.tensor_copy(part[1], left))
                if k == 3:
                    then(dve.tensor_tensor(left, left, part[1], ALU.subtract))
                if k == 4:
                    dve.memset(x_parts[:, lo:hi, PARTS * F:XP], 1.0)
                    dve.tensor_copy(part[2], left).then_inc(parts_done, 1)

            for L in range(3):
                a = SLOPES[L]
                if L > 0:
                    dve.wait_ge(pv_done, DEEP + KT * L)
                    dve.wait_ge(prep_done, NP * L)
                if L == 0:
                    for n in PROJ[L]:
                        with dve.Fori(0, NG // PD) as g4:
                            take_projected(L, n, g4)
                else:
                    n, = PROJ[L]
                    last_fin = (NP - PQ + 1) * (L - 1) + LAST_FIN
                    recip(SB, last_fin)
                    take_projected(L, n, 0)
                    sums(SB, last_fin)
                    take_projected(L, n, 1)
                    squares(SB, last_fin)
                    with dve.Fori(2, NG // PD) as g4:
                        take_projected(L, n, g4)
                dve.wait_ge(proj_done, PD + NG * (PROJ[L][-1] + 1))
                dve.tensor_scalar(d_col[:, :], s_col[:, :], 1.0 - a, None, ALU.mult)
                dve.tensor_scalar(as_col[:, :], s_col[:, :], a, None, ALU.mult)
                dve.tensor_scalar(c_col[:, :], t_col[:, :], a - 1.0, None, ALU.mult)
                dve.tensor_reduce(t_abs[:, :], t_col[:, :], AX_X, ALU.max, apply_absolute_value=True)\
                   .then_inc(abs_done, 1)
                dve.wait_ge(abs_t_done, L + 1)
                then(dve.tensor_reduce(t_top[:, 0:1], col_ps[0:1, 0:P], AX_X, ALU.max))
                then(dve.tensor_scalar(t_top[:, 0:1], t_top[:, 0:1], TINY, None, ALU.max))
                dve.tensor_scalar(t_top[:, 1:2].bitcast(I32), t_top[:, 0:1].bitcast(I32), 0x7F800000, None,
                                  ALU.bitwise_and).then_inc(top_done, 1)
                dve.wait_ge(scale_ps_done, L + 1)
                then(dve.tensor_copy(scale_col[:, :], col_ps[:, 256:257]))
                then(dve.reciprocal(unscale[:, :], scale_col[:, :]))
                then(dve.tensor_scalar(tn_col[:, :], t_col[:, :], unscale[:, 0:1], None, ALU.mult))
                dve.memset(e_small[:, 7, :], 0.0).then_inc(cols_done, 1)
                with dve.Fori(0, NG // PD) as g4:
                    for i in range(PD):
                        g = PD * g4 + i
                        dve.wait_ge(trow_ps_done, NG * L + g + 1)
                        dve.tensor_tensor(t_diag[:, i, :, :], ident[:, :].unsqueeze(1).to_broadcast([P, GB, P]),
                                          tn_col[:, bass.ds(GB * g, GB)].unsqueeze(2).to_broadcast([P, GB, P]),
                                          ALU.mult).then_inc(diag_done, 1)
                dve.wait_ge(trow_done, PD + NG * (L + 1))
                with dve.Fori(0, AHEAD) as pair:
                    for i in range(2):
                        for c in range(NQ):
                            row_max_quarter(L, 2 * pair + i, c, i)
                    pair_max_out(L, pair)
                fins = (NP - PQ + 1) * L

                def switch(s):
                    dve.tensor_copy(s2_mask[0:PARTS, :], s2_ring[:, bass.ds(W * (s % 2), W)]).then_inc(switched, 1)

                dve.wait_ge(prep_rows_done, 2 * (NP * L + PQ))
                switch(0)

                def body(q, row_max_on, prepare, finish, opens, closes, L=L, fins=fins):
                    for u in range(UN):
                        k = UN * q + u
                        dve.wait_ge(mask_ps_done, KT * L + k + 1)
                        dve.wait_ge(exp_done, KT * L + k + 1)
                        if closes is not None and not ends(closes) and u == UN - 1:
                            dve.wait_ge(prep_rows_done, 2 * (NP * L + PQ + 1 + q))
                            switch(closes)
                        dve.scalar_tensor_tensor(out=score[:, u % DEEP, :], in0=d_row[:, bass.ds(W * (q // PQ % 2), W)],
                                                 scalar=c_col[:, bass.ds(k % NB, 1)], in1=z_ps[:, u % 2, :],
                                                 op0=ALU.max, op1=ALU.add).then_inc(score_done, 1)
                        if row_max_on and u % 2:
                            i, c = u // SB, (u % SB) // 2
                            row_max_quarter(L, 2 * (q + AHEAD) + i, c, i)
                        if finish:
                            count = fins + q - PQ
                            if u == 7:
                                recip(2, count)
                            if u == 12:
                                sums(2, count)
                            if u == 15:
                                squares(2, count)
                        if L == 2 and ends(closes) and u % 3 == 1 and u // 3 < PART_OPS:
                            if u == 1:
                                dve.wait_ge(x_done, fins + EARLY // 2)
                            part_step(u // 3, 0, EARLY)
                    if row_max_on:
                        pair_max_out(L, q + AHEAD)

                layer_loop(dve, body, lambda s: None, L)
            last_fin = 2 * (NP - PQ + 1) + LAST_FIN
            def to_bf16(jc, s2, i):
                g = NS * jc + 2 * s2 + i
                dve.wait_ge(chunk_in[i], 16 * (3 * CH_BASE + (NS // 2) * jc + s2 + 1))
                dve.wait_ge(agg_step, g + 1)
                dve.tensor_scalar(adj_b[:, i, SB // 2:SB, :], chunk[:, i, SB // 2:SB, :], 0.0, None,
                                  ALU.is_ge).then_inc(adj_done, 1)

            def beside(g):
                if g == 0:
                    recip(SB, last_fin)
                if g == 2:
                    sums(SB, last_fin)
                if g == 3:
                    squares(SB, last_fin)
                    dve.wait_ge(x_done, fins3)
                    for k in range(PART_OPS):
                        part_step(k, EARLY, NB)

            base = steps[0] + PART_OPS - 1

            def finish_columns(jc, k):
                count = fins3 + jc
                if k == 0:
                    dve.wait_ge(agg_done, 4 * jc + 4)
                    dve.reciprocal(e_small[:, 0, :], acc3[:, :, PARTS * F]).then_inc(dve_step, 1)
                    dve.wait_ge(dve_step, base + 2 * jc + 1)
                    dve.tensor_scalar(e_small[:, 6, :], e_small[:, 0, :], 0.0, None, ALU.mult)
                if k == 2:
                    dve.wait_ge(lin_ps_done, jc + 1)
                    dve.tensor_tensor(e_o[:, :, :], col_ps[:, :].rearrange("p (b f) -> p b f", b=SB),
                                      e_small[:, 0, :].unsqueeze(2).to_broadcast([P, SB, F]), ALU.mult)\
                       .then_inc(dve_step, 1)
                    dve.wait_ge(dve_step, base + 2 * jc + 2)
                    dve.scalar_tensor_tensor(out=e_o[:, :, :], in0=e_o[:, :, :], scalar=0.0,
                                             in1=x_cur[:, bass.ds(SB * jc, SB), :], op0=ALU.max, op1=ALU.add)\
                       .then_inc(relu_done, 1)
                    dve.wait_ge(relu_done, jc + 1)
                    dve.tensor_reduce(e_small[:, 1, :], e_o[:, :, :], AX_X, ALU.add).then_inc(sum_done, 1)
                if k == 3:
                    dve.wait_ge(sq_done, count + 1)
                    dve.tensor_reduce(e_small[:, 3, :], e_x[:, :, :], AX_X, ALU.add).then_inc(var_done, 1)

            layer3_loop(dve, to_bf16, finish_columns, beside)
            assert steps[0] == base

        @block.tensor
        def _(pe):
            pe.sem_inc(xt_ps_done, PD)
            pe.sem_inc(proj_ps_done, PD)
            pe.sem_inc(trow_ps_done, PD)
            pe.sem_inc(pv_done, DEEP)
            pe.sem_inc(agg_step, PRIME)
            pe.wait_ge(inputs_in, 16 * 11)
            pe.wait_ge(consts_done, 6)
            for l in range(3):
                last = pe.transpose(col_ps[0:F, F * l:F * l + F], proj[:, l, 0:F], ident[0:F, 0:F])
            last.then_inc(wt_ps_done, 1)
            pe.wait_ge(wt_done, 1)
            for l in range(3):
                last = pe.matmul(row_ps[0:F, 2 * l:2 * l + 2], wgt_t[:, l, :], a_cols[:, l, :], start=True, stop=True)
            last.then_inc(wa_ps_done, 1)
            pe.wait_ge(consts_cast, 1 + 1 + W // BANK * HB + 1)

            def prepare_rows(L, pi, closed):
                pe.wait_ge(prep_done, NP * L + pi + 1)
                pe.wait_ge(prep_rows_done, 2 * (NP * L + pi))
                pe.wait_ge(acc_done, 2 * (NS * L + closed))
                pe.matmul(col_ps[:, 0:2 * P], ones[:, :], d_diag[:, :, :].rearrange("p b n -> p (b n)"),
                          start=True, stop=True)
                for b in range(2):
                    last = pe.transpose(row_ps_b[0:PARTS, P * b:P * b + P], s2_parts[:, b, :], ident_b[:, :])
                last.then_inc(prep_ps_done, 1)

            def mask_tile(L, q, u, first_of_chunk):
                k = UN * q + u
                if first_of_chunk:
                    wait_alone(pe, chunk_in[u // SB], 48 * ((NS * NS // 2) * L + q + 1))
                wait_alone(pe, score_done, KT * L + k + 1)
                for half in range(W // BANK):
                    for b in range(HB):
                        at = BANK * half + MB * b
                        width = min(MB, BANK * (half + 1) - at)
                        last = pe.matmul(z_ps[:, u % 2, at:at + width],
                                         edges8[0:PARTS + width, u // SB, HB * half + b, P * (u % SB):P * (u % SB) + P],
                                         s2_mask[0:PARTS + width, at:at + width], start=True, stop=True)
                last.then_inc(mask_ps_done, 1)

            def add_tile(L, q, u):
                k = UN * q + u
                if u % SB == 0:
                    wait_alone(pe, h_staged, NS * NS * L + 2 * q + u // SB + 1)
                pe.wait_ge(exp_done, DEEP + KT * L + k + 1)
                for i in range(2):
                    last = pe.matmul(acc_ps[0:FA, i, :], h_tiles[:, u // SB, u % SB, :],
                                     prob[:, u % DEEP, 512 * i:512 * i + 512], start=False, stop=False,
                                     skip_group_check=True)
                last.then_inc(pv_done, 1)

            def clear(banks, width):
                for bank in banks:
                    pe.matmul(bank, zeros_b[:, 0:bank.shape[0]], zeros_b[:, 0:width], start=True, stop=False,
                              skip_group_check=True)

            for L in range(3):
                for n in PROJ[L]:
                    l = L
                    with pe.Fori(0, NG // PD) as g4:
                        for i in range(PD):
                            g = PD * g4 + i
                            wait_alone(pe, stage_done, NG * n + g + 1)
                            wait_alone(pe, xt_done, NG * n + g + 1)
                            for b in range(GB):
                                last = pe.transpose(xt_ps[0:F, i, P * b:P * b + P], stage[:, i, F * b:F * b + F],
                                                    ident[:, :])
                            last.then_inc(xt_ps_done, 1)
                        for i in range(PD):
                            g = PD * g4 + i
                            wait_alone(pe, xt_done, PD + NG * n + g + 1)
                            wait_alone(pe, proj_done, NG * n + g + 1)
                            for b in range(GB):
                                last = pe.matmul(proj_ps[i][:, (F + 2) * b:(F + 2) * (b + 1)],
                                                 xt_sb[:, i, P * b:P * b + P], proj[:, l, :], start=True, stop=True)
                            last.then_inc(proj_ps_done, 1)
                pe.wait_ge(abs_done, L + 1)
                pe.wait_ge(prep_rows_done, 2 * NP * L)
                pe.transpose(col_ps[0:1, 0:P], t_abs[:, :], ident[:, :]).then_inc(abs_t_done, 1)
                pe.wait_ge(top_done, L + 1)
                pe.matmul(col_ps[:, 256:257], ones[0:1, :], t_top[:, 1:2], start=True, stop=True)\
                  .then_inc(scale_ps_done, 1)
                with pe.Fori(0, NG // PD) as g4:
                    for i in range(PD):
                        g = PD * g4 + i
                        pe.wait_ge(diag_done, NG * L + g + 1)
                        pe.wait_ge(trow_done, NG * L + g + 1)
                        pe.matmul(xt_ps[:, i, :], ones[:, :], t_diag[:, i, :, :].rearrange("p b n -> p (b n)"),
                                  start=True, stop=True).then_inc(trow_ps_done, 1)
                clear([acc_ps[:, 0, 0:FA]], FA)
                with pe.Fori(0, NB - 1) as b:
                    pe.matmul(acc_ps[:, 0, 0:FA], ones[:, :], h_aug[:, bass.ds(b, 1), :]
                              .rearrange("p a f -> p (a f)"), start=False, stop=False, skip_group_check=True)
                pe.matmul(acc_ps[:, 0, 0:FA], ones[:, :], h_aug[:, NB - 1, :], start=False, stop=True,
                          skip_group_check=True).then_inc(hsum_ps_done, 1)
                with pe.Fori(0, PQ) as pi:
                    prepare_rows(L, pi, 0)

                pe.wait_ge(switched, NS * L + 1)
                pe.wait_ge(trow_done, PD + NG * (L + 1))
                pe.wait_ge(hsum_done, L + 1)
                clear([acc_ps[0:FA, i, :] for i in range(2)], 512)
                for u in range(LAG):
                    mask_tile(L, 0, u, u == 0)

                def body(q, row_max_on, prepare, finish, opens, closes, L=L):
                    for u in range(UN):
                        add_tile(L, q, u)
                        if opens is not None and u == 1:
                            turn(opens - 1)
                        if prepare and u == 8:
                            prepare_rows(L, q + PQ, q // PQ)
                        ahead = u + LAG
                        if opens is not None and u == 0:
                            continue
                        if ahead < UN:
                            mask_tile(L, q, ahead, ahead % SB == 0)
                        elif not ends(closes):
                            if closes is not None and ahead == UN:
                                wait_alone(pe, switched, NS * L + closes + 1)
                            mask_tile(L, q + 1, ahead - UN, ahead == UN)
                    if closes is not None and not ends(closes):
                        mask_tile(L, q + 1, LAG, False)

                def close(s, L=L):
                    pe.wait_ge(acc_t_done, 2 * (NS * L) + 2 * (s + 1))
                    if not (isinstance(s, int) and s == NS - 1):
                        clear([acc_ps[0:FA, i, :] for i in range(2)], 512)

                def turn(s, L=L):
                    ready = PQ * (s + 2)
                    pe.wait_ge(prep_rows_done, 2 * (NP * L + (min(ready, NP) if isinstance(s, int) else ready)))
                    for i in range(2):
                        for b in range(SB // 2):
                            at = P * (SB // 2 * i + b)
                            last = pe.transpose(turned[i][:, FA * b:FA * b + FA], acc_t[:, at:at + P],
                                                ident[0:FA, 0:FA])
                        last.then_inc(turned_done, 1)

                layer_loop(pe, body, close, L)
                turn(NS - 1)

            pe.wait_ge(parts_done, 1)
            pe.wait_ge(score_done, PRIME + 3 * KT)

            def add_chunk(jc, s2, i):
                g = NS * jc + 2 * s2 + i
                if isinstance(s2, int) and s2 == 0 and i == 0:
                    if not isinstance(jc, int):
                        pe.wait_ge(agg_done, 4 * jc)
                    clear([z_flat[:, 512 * k:512 * k + 2 * XP] for k in range(4)], 2 * XP)
                if isinstance(jc, int) and isinstance(s2, int) and (2 * s2 + i) * SB == EARLY:
                    pe.wait_ge(parts_done, 2)
                pe.wait_ge(adj_done, PRIME + g + 1)
                pe.wait_ge(adj_done_a, PRIME + g + 1)
                for b in range(SB):
                    for j in range(SB):
                        at = 512 * (j // 2) + XP * (j % 2)
                        last = pe.matmul(z_flat[:, at:at + XP], adj_b[:, i, b, P * j:P * j + P],
                                         x_parts[:, bass.ds(SB * (2 * s2 + i) + b, 1), 0:XP]
                                         .rearrange("p a n -> p (a n)"), start=False, stop=False,
                                         skip_group_check=True)
                last.then_inc(agg_step, 1)

            def turn_and_multiply(jc, k):
                if k == 0:
                    wait_alone(pe, agg_sum, jc + 1)
                    for i in range(2):
                        for b in range(4):
                            last = pe.transpose(acc_ps[0:F, i, P * b:P * b + P], agg_sb[:, 4 * i + b, :], ident[:, :])
                        last.then_inc(aggt_ps_done, 1)
                if k == 1:
                    pe.wait_ge(relu_done, jc)
                    for i in range(2):
                        pe.wait_ge(aggt_done, 2 * jc + i + 1)
                        for b in range(4):
                            last = pe.matmul(col_ps[:, F * (4 * i + b):F * (4 * i + b + 1)],
                                             aggt_sb[:, i, P * b:P * b + P], ut[:, :], start=True, stop=True)
                    last.then_inc(lin_ps_done, 1)

            layer3_loop(pe, add_chunk, turn_and_multiply)


_INS = ['x', 'adj', 'L0_gnn_entity_embs', 'L0_gnn_W', 'L0_gnn_a', 'L1_gnn_W', 'L1_gnn_a', 'L2_gnn_W', 'L2_gnn_a',
        'L3_gnn_U']


def kernel(**inputs):
    import numpy as _np
    import concourse.bacc as _bacc
    from concourse import mybir as _mybir
    from concourse.bass_utils import run_bass_kernel_spmd as _run

    nc = _bacc.Bacc("TRN2", target_bir_lowering=False, num_devices=1)
    arrays, args = {}, []
    for name in _INS:
        a = _np.asarray(inputs[name])
        a = _np.ascontiguousarray(a.T if name == 'L3_gnn_U' else a)
        arrays[f"in_{name}"] = a
        args.append(nc.dram_tensor(f"in_{name}", a.shape, _mybir.dt.from_np(a.dtype), kind="ExternalInput").ap())
    shape = arrays["in_x"].shape
    args.append(nc.dram_tensor("out_x", shape, _mybir.dt.from_np(_np.dtype("float32")), kind="ExternalOutput").ap())
    build(nc, *args)
    r = _run(nc, [arrays], core_ids=[0])
    return r.results[0]["out_x"]
```
